# Optimizing a Trainium2 kernel written in Bass

```python
import numpy as np
import jax
import jax.numpy as jnp

def _softmax(x, axis=-1):
    return jax.nn.softmax(x, axis=axis)

def _gelu(x):
    return jax.nn.gelu(x, approximate=True)

def _silu(x):
    return jax.nn.silu(x)

def _sigmoid(x):
    return jax.nn.sigmoid(x)

def _layernorm(x, axis=-1, eps=1e-05):
    m = jnp.mean(x, axis=axis, keepdims=True)
    v = jnp.var(x, axis=axis, keepdims=True)
    return (x - m) / jnp.sqrt(v + eps)

def _scatter_add(tgt, idx, src, axis=0):
    return tgt.at[idx].add(src)

def _segment_sum(src, seg, n):
    return jax.ops.segment_sum(src, seg, n)
kernel_name = 'mk_flamingo_gated_d1_seqx_r8_a998d9'

def setup_inputs(seed: int=0):
    np.random.seed(seed)
    _w = jnp.asarray

    def _rec_inputs():
        import jax
        import jax.numpy as jnp
        _rk = jax.random.key(seed)
        x = 4.136e-05 + 0.9999 * jax.random.normal(jax.random.fold_in(_rk, 1), (4, 256, 256), jnp.float32)
        _lenS = 256 - jax.random.randint(jax.random.fold_in(_rk, 7), (4,), 0, max(1, 256 // 4) + 1, jnp.int32)
        _lenS2 = 256 - jax.random.randint(jax.random.fold_in(_rk, 8), (4,), 0, max(1, 256 // 4) + 1, jnp.int32)
        _ctx_1024P = jax.random.normal(jax.random.fold_in(_rk, 11), (4, 16, 128), jnp.float32)
        _ctx_1024c = jax.random.dirichlet(jax.random.fold_in(_rk, 511), 0.3 * jnp.ones((16,), jnp.float32), (4, 256))
        _ctx_1024t = jnp.einsum('bsk,bkd->bsd', _ctx_1024c, _ctx_1024P)
        _ctx_1024t = _ctx_1024t * jax.lax.rsqrt(jnp.mean(jnp.square(_ctx_1024t)) + 1e-12) * 0.953939
        ctx_1024 = -0.000292821 + 1.00034 * (_ctx_1024t + 0.3 * jax.random.normal(jax.random.fold_in(_rk, 611), (4, 256, 128), jnp.float32))
        _g = jax.random.normal(jax.random.fold_in(_rk, 9001), (2, 1), jnp.float32)
        _g = jnp.sign(_g) * jnp.maximum(jnp.abs(_g), 1.0) + (_g == 0) * 1.0
        g_xattn = _g[0]
        g_ffn = _g[1]
        return (x, ctx_1024, g_xattn, g_ffn)
    x, ctx_1024, g_xattn, g_ffn = _rec_inputs()

    def _L0_xattn_setup():
        import jax, jax.numpy as jnp
        import numpy as np
        import math
        B, L, DM = (2, 256, 128)
        DS, DC, EXP = (16, 4, 2)
        DI = EXP * DM
        DR = math.ceil(DM / 16)
        DT_MIN, DT_MAX, DT_FLOOR = (0.001, 0.1, 0.0001)

        def _ssm_forward(hidden_states, z, in_proj_w, conv_w, conv_b, x_proj_w, dt_proj_w, dt_proj_b, A_log, D):
            b = hidden_states.shape[0]
            x = jnp.einsum('ed,bld->bel', in_proj_w, hidden_states)
            xp = jnp.pad(x, ((0, 0), (0, 0), (DC - 1, 0)))
            xc = jax.lax.conv_general_dilated(xp, conv_w[:, None, :], window_strides=(1,), padding='VALID', dimension_numbers=('NCH', 'OIH', 'NCH'), feature_group_count=DI)
            u = jax.nn.silu(xc + conv_b[None, :, None])
            x_dbl = jnp.einsum('ke,bel->bkl', x_proj_w, u)
            dt_lo = x_dbl[:, :DR]
            Bm = x_dbl[:, DR:DR + DS]
            Cm = x_dbl[:, DR + DS:]
            delta = jax.nn.softplus(jnp.einsum('er,brl->bel', dt_proj_w, dt_lo) + dt_proj_b[None, :, None])
            A = -jnp.exp(A_log)

            def step(state, xs):
                d_t, B_t, C_t, u_t = xs
                dA = jnp.exp(d_t[..., None] * A)
                state = state * dA + (d_t * u_t)[..., None] * B_t[:, None, :]
                y_t = jnp.einsum('ben,bn->be', state, C_t)
                return (state, y_t)
            xs = (jnp.moveaxis(delta, -1, 0), jnp.moveaxis(Bm, -1, 0), jnp.moveaxis(Cm, -1, 0), jnp.moveaxis(u, -1, 0))
            state0 = jnp.zeros((b, DI, DS), delta.dtype)
            _, ys = jax.lax.scan(step, state0, xs)
            y = jnp.moveaxis(ys, 0, -1)
            y = y + D[None, :, None] * u
            y = y * jax.nn.silu(z)
            return jnp.swapaxes(y, 1, 2)
        key = jax.random.key(seed)
        ks = jax.random.split(key, 8)
        hidden_states = jax.random.normal(ks[0], (B, L, DM), jnp.float32)
        z = jax.random.normal(ks[1], (B, DI, L), jnp.float32)
        in_proj_w = jax.random.normal(ks[2], (DI, DM), jnp.float32) * DM ** (-0.5)
        conv_w = jax.random.normal(ks[3], (DI, DC), jnp.float32) * DC ** (-0.5)
        conv_b = jnp.zeros((DI,), jnp.float32)
        x_proj_w = jax.random.normal(ks[4], (DR + 2 * DS, DI), jnp.float32) * DI ** (-0.5)
        dt_std = DR ** (-0.5)
        dt_proj_w = jax.random.uniform(ks[5], (DI, DR), jnp.float32, -dt_std, dt_std)
        dt = jnp.exp(jax.random.uniform(ks[6], (DI,), jnp.float32) * (math.log(DT_MAX) - math.log(DT_MIN)) + math.log(DT_MIN))
        dt = jnp.clip(dt, DT_FLOOR)
        dt_proj_b = dt + jnp.log(-jnp.expm1(-dt))
        A_log = jnp.log(jnp.broadcast_to(jnp.arange(1, DS + 1, dtype=jnp.float32), (DI, DS)))
        D = jnp.ones((DI,), jnp.float32)
        return dict(hidden_states=hidden_states, z=z, in_proj_w=in_proj_w, conv_w=conv_w, conv_b=conv_b, x_proj_w=x_proj_w, dt_proj_w=dt_proj_w, dt_proj_b=dt_proj_b, A_log=A_log, D=D)
    _L0_xattn_all = _L0_xattn_setup()
    _L0_xattn_in = {k: v for k, v in _L0_xattn_all.items() if k in ('in_proj_w', 'conv_w', 'conv_b', 'x_proj_w', 'dt_proj_w', 'dt_proj_b', 'A_log', 'D')}
    del _L0_xattn_all

    def _L0_ffn_setup():
        import jax, jax.numpy as jnp
        import numpy as np
        B, S, D, M, E, K = (4, 256, 256, 512, 8, 2)

        def _routed_moe(x, gate_w, w0, w1, wo):
            T = x.shape[0]
            logits = jnp.einsum('td,de->te', x, gate_w)
            top_logits, top_idx = jax.lax.top_k(logits, K)
            top_w = jax.nn.softmax(top_logits, axis=-1)
            cw = jnp.zeros((T, E), dtype=x.dtype).at[jnp.arange(T)[:, None], top_idx].add(top_w)
            out = jnp.zeros_like(x)
            for e in range(E):
                h = jax.nn.silu(x @ w0[e]) * (x @ w1[e])
                out = out + cw[:, e:e + 1] * (h @ wo[e])
            return out
        key = jax.random.key(seed)
        ks = jax.random.split(key, 5)
        inputs = jax.random.normal(ks[0], (B, S, D), dtype=jnp.float32)
        gate_w = jax.random.normal(ks[1], (D, E), dtype=jnp.float32) * D ** (-0.5)
        w0 = jax.random.normal(ks[2], (E, D, M), dtype=jnp.float32) * D ** (-0.5)
        w1 = jax.random.normal(ks[3], (E, D, M), dtype=jnp.float32) * D ** (-0.5)
        wo = jax.random.normal(ks[4], (E, M, D), dtype=jnp.float32) * M ** (-0.5)
        decoder_segment_ids = jax.random.randint(jax.random.fold_in(key, 1), (B, S), 0, 2).astype(jnp.int32)
        decoder_positions = jnp.tile(jnp.arange(S, dtype=jnp.int32)[None, :], (B, 1))
        return {'inputs': inputs, 'gate_w': gate_w, 'w0': w0, 'w1': w1, 'wo': wo, 'decoder_segment_ids': decoder_segment_ids, 'decoder_positions': decoder_positions}
    _L0_ffn_all = _L0_ffn_setup()
    _L0_ffn_in = {k: v for k, v in _L0_ffn_all.items() if k in ('gate_w', 'w0', 'w1', 'wo', 'decoder_segment_ids', 'decoder_positions')}
    del _L0_ffn_all
    return {'x': x, 'ctx_1024': ctx_1024, 'g_xattn': g_xattn, 'g_ffn': g_ffn, 'L0_xattn_in_proj_w': _L0_xattn_in['in_proj_w'], 'L0_xattn_conv_w': _L0_xattn_in['conv_w'], 'L0_xattn_conv_b': _L0_xattn_in['conv_b'], 'L0_xattn_x_proj_w': _L0_xattn_in['x_proj_w'], 'L0_xattn_dt_proj_w': _L0_xattn_in['dt_proj_w'], 'L0_xattn_dt_proj_b': _L0_xattn_in['dt_proj_b'], 'L0_xattn_A_log': _L0_xattn_in['A_log'], 'L0_xattn_D': _L0_xattn_in['D'], 'L0_ffn_gate_w': _L0_ffn_in['gate_w'], 'L0_ffn_w0': _L0_ffn_in['w0'], 'L0_ffn_w1': _L0_ffn_in['w1'], 'L0_ffn_wo': _L0_ffn_in['wo'], 'L0_ffn_decoder_segment_ids': _L0_ffn_in['decoder_segment_ids'], 'L0_ffn_decoder_positions': _L0_ffn_in['decoder_positions']}

def reference(x, ctx_1024, g_xattn, g_ffn, L0_xattn_in_proj_w, L0_xattn_conv_w, L0_xattn_conv_b, L0_xattn_x_proj_w, L0_xattn_dt_proj_w, L0_xattn_dt_proj_b, L0_xattn_A_log, L0_xattn_D, L0_ffn_gate_w, L0_ffn_w0, L0_ffn_w1, L0_ffn_wo, L0_ffn_decoder_segment_ids, L0_ffn_decoder_positions):
    import jax
    import jax.numpy as jnp

    def _L0_xattn_ref(hidden_states, z, in_proj_w, conv_w, conv_b, x_proj_w, dt_proj_w, dt_proj_b, A_log, D):
        import jax, jax.numpy as jnp
        import numpy as np
        import math
        B, L, DM = (2, 256, 128)
        DS, DC, EXP = (16, 4, 2)
        DI = EXP * DM
        DR = math.ceil(DM / 16)
        DT_MIN, DT_MAX, DT_FLOOR = (0.001, 0.1, 0.0001)

        def _ssm_forward(hidden_states, z, in_proj_w, conv_w, conv_b, x_proj_w, dt_proj_w, dt_proj_b, A_log, D):
            b = hidden_states.shape[0]
            x = jnp.einsum('ed,bld->bel', in_proj_w, hidden_states)
            xp = jnp.pad(x, ((0, 0), (0, 0), (DC - 1, 0)))
            xc = jax.lax.conv_general_dilated(xp, conv_w[:, None, :], window_strides=(1,), padding='VALID', dimension_numbers=('NCH', 'OIH', 'NCH'), feature_group_count=DI)
            u = jax.nn.silu(xc + conv_b[None, :, None])
            x_dbl = jnp.einsum('ke,bel->bkl', x_proj_w, u)
            dt_lo = x_dbl[:, :DR]
            Bm = x_dbl[:, DR:DR + DS]
            Cm = x_dbl[:, DR + DS:]
            delta = jax.nn.softplus(jnp.einsum('er,brl->bel', dt_proj_w, dt_lo) + dt_proj_b[None, :, None])
            A = -jnp.exp(A_log)

            def step(state, xs):
                d_t, B_t, C_t, u_t = xs
                dA = jnp.exp(d_t[..., None] * A)
                state = state * dA + (d_t * u_t)[..., None] * B_t[:, None, :]
                y_t = jnp.einsum('ben,bn->be', state, C_t)
                return (state, y_t)
            xs = (jnp.moveaxis(delta, -1, 0), jnp.moveaxis(Bm, -1, 0), jnp.moveaxis(Cm, -1, 0), jnp.moveaxis(u, -1, 0))
            state0 = jnp.zeros((b, DI, DS), delta.dtype)
            _, ys = jax.lax.scan(step, state0, xs)
            y = jnp.moveaxis(ys, 0, -1)
            y = y + D[None, :, None] * u
            y = y * jax.nn.silu(z)
            return jnp.swapaxes(y, 1, 2)
        return _ssm_forward(hidden_states, z, in_proj_w, conv_w, conv_b, x_proj_w, dt_proj_w, dt_proj_b, A_log, D)

    def _L0_ffn_ref(inputs, gate_w, w0, w1, wo, decoder_segment_ids, decoder_positions):
        import jax, jax.numpy as jnp
        import numpy as np
        B, S, D, M, E, K = (4, 256, 256, 512, 8, 2)

        def _routed_moe(x, gate_w, w0, w1, wo):
            T = x.shape[0]
            logits = jnp.einsum('td,de->te', x, gate_w)
            top_logits, top_idx = jax.lax.top_k(logits, K)
            top_w = jax.nn.softmax(top_logits, axis=-1)
            cw = jnp.zeros((T, E), dtype=x.dtype).at[jnp.arange(T)[:, None], top_idx].add(top_w)
            out = jnp.zeros_like(x)
            for e in range(E):
                h = jax.nn.silu(x @ w0[e]) * (x @ w1[e])
                out = out + cw[:, e:e + 1] * (h @ wo[e])
            return out
        b, s, d = inputs.shape
        x = inputs.reshape(b * s, d)
        out = _routed_moe(x, gate_w, w0, w1, wo)
        return out.reshape(b, s, d)
    x = x + jnp.tanh(g_xattn[0]) * _L0_xattn_ref(ctx_1024, _layernorm(x, axis=-1), L0_xattn_in_proj_w, L0_xattn_conv_w, L0_xattn_conv_b, L0_xattn_x_proj_w, L0_xattn_dt_proj_w, L0_xattn_dt_proj_b, L0_xattn_A_log, L0_xattn_D)
    x = x + jnp.tanh(g_ffn[0]) * _L0_ffn_ref(_layernorm(x, axis=-1), L0_ffn_gate_w, L0_ffn_w0, L0_ffn_w1, L0_ffn_wo, L0_ffn_decoder_segment_ids, L0_ffn_decoder_positions)
    return x

_drawn_inputs = setup_inputs


def setup_inputs(seed=0):
    import zlib

    import numpy as np

    out = dict(_drawn_inputs(seed))
    spreads = {'L0_xattn_conv_b': (0.0, 0.1), 'L0_xattn_D': (1.0, 0.2)}
    factors = {}
    for name, (base, spread) in spreads.items():
        noise = np.random.default_rng([zlib.crc32(name.encode()), seed]).standard_normal(out[name].shape)
        drawn = base * np.exp(spread * noise) if base else spread * noise
        out[name] = jnp.asarray(drawn.astype(out[name].dtype))
    for name, factor in factors.items():
        out[name] = (out[name] * factor).astype(out[name].dtype)
    return out
```

```python
from contextlib import ExitStack

import numpy as np

import concourse.bass as bass
from concourse import mybir

F32 = mybir.dt.float32
F32R = mybir.dt.float32r
I32 = mybir.dt.int32
U32 = mybir.dt.uint32
ALU = mybir.AluOpType
ACT = mybir.ActivationFunctionType
AX_X = mybir.AxisListType.X

P = 128
B, L, DX = 4, 256, 256
DM, DI, DS, DC, DR = 128, 256, 16, 4, 8
E, MH, TOPK = 8, 512, 2
TOK = B * L
NBLK = TOK // P
NQ = 2
QB = B // NQ
QT = QB * L
QBLK = QT // P
CH = P // DS
GRP = 64
NG = DI // GRP
TPG = GRP // CH
NTILE = NQ * NG * TPG
SLOTS = (TOK * TOPK - E) // P + E
EPS = 1e-5
AHEAD = 2


def build(nc, x, ctx_1024, g_xattn, g_ffn, in_proj_w, conv_w, conv_b, x_proj_w, dt_proj_w, dt_proj_b,
          A_log, D, gate_w, w0, w1, wo, out):
    stack = ExitStack()
    with stack:
        def sb(name, shape, dt=F32):
            return stack.enter_context(nc.sbuf_tensor(name, shape, dt))

        def sem(name):
            return stack.enter_context(nc.semaphore(name))

        W0 = sb("W0", [P, E, 2, MH])
        W1 = sb("W1", [P, E, 2, MH])
        WO = sb("WO", [P, E, 4, DX])
        early = WO[:, :, :, :].rearrange("p e k n -> p (e k n)")
        taken = [0]

        def early_part(n):
            taken[0] += n
            return early[:, taken[0] - n:taken[0]]

        ctx_sb = early_part(NBLK * DM).rearrange("p (t d) -> p t d", t=NBLK)
        ctxT = early_part(B * (L + DC - 1)).rearrange("p (b l) -> p b l", b=B)
        tapw = early_part(2 * DC * DM).rearrange("p (h k d) -> p h k d", h=2, k=DC)
        tapwT = early_part(2 * DC * P).rearrange("p (h k e) -> p h k e", h=2, k=DC)
        spread_f = early_part(TPG * P)
        sp_relu = early_part(QT)
        sp_exp = early_part(QT)
        sp_ln = early_part(QT)
        sp_rest = early_part(QT)
        inw = early_part(2 * DM).rearrange("p (h d) -> p h d", h=2)
        assert taken[0] <= E * 4 * DX

        d_parts = sb("d_parts", [P, NQ * NG, QT], F32R)
        du_parts = sb("du_parts", [P, NQ * NG, QT], F32R)
        B_rep = sb("B_rep", [P, NQ, QT])
        C_rep = sb("C_rep", [P, NQ, QT])
        dA = sb("dA", [P, 2, QT])
        dBu = sb("dBu", [P, 2, QT])
        hst = sb("hst", [P, 2, QT])
        hC = sb("hC", [P, 2, QT])
        u = sb("u", [P, NQ, 2, QT])
        xs = sb("xs", [P, NBLK, DX])
        zT = sb("zT", [P, NBLK, DX])
        spread = sb("spread", [P, TPG, P], F32R)
        gather8 = sb("gather8", [P, CH])
        ident = sb("ident", [P, P])
        ones = sb("ones", [P, P])
        before = sb("before", [P, P])
        diagD = sb("diagD", [P, 2, P])
        Aneg = sb("Aneg", [P, NQ * NG * TPG])
        Aexp = sb("Aexp", [P, NG * TPG])
        Alog_sb = sb("Alog_sb", [NG * TPG, P])
        xproj_sb = sb("xproj_sb", [DR + 2 * DS, DI])
        xprojT_B = sb("xprojT_B", [P, 2, CH, DS])
        xprojT_C = sb("xprojT_C", [P, 2, CH, DS])
        xprojT_dt = sb("xprojT_dt", [P, 2, DR])
        dtw_sb = sb("dtw_sb", [P, 2, DR])
        dtwT = sb("dtwT", [DR, 2, P])
        dt_lo = sb("dt_lo", [DR, NQ, QT])
        convw = sb("convw", [P, 2, DC])
        cols = sb("cols", [P, 3, 2])
        vec_rows = sb("vec_rows", [6, P])
        gates = sb("gates", [P, 2])
        tg = sb("tg", [P, 2])
        stats = sb("stats", [P, 2, NBLK, 6])
        mv = sb("mv", [P, 2, NBLK, 2])
        vare = sb("vare", [P, 2, NBLK])
        std = sb("std", [P, 2, NBLK])
        rstd = sb("rstd", [P, 2, NBLK])
        nmr = sb("nmr", [P, NBLK])
        gate_sb = sb("gate_sb", [P, 2, E])
        xnT = sb("xnT", [P, QBLK, 2, P])
        logits = sb("logits", [P, NBLK, E])
        top = sb("top", [P, NBLK, 8])
        topi = sb("topi", [P, NBLK, 8], U32)
        topf = sb("topf", [P, TOPK, NBLK])
        iota_e = sb("iota_e", [P, NBLK, E])
        hot = sb("hot", [P, TOPK, NBLK, E])
        mask = sb("mask", [P, NBLK, E])
        rank = sb("rank", [P, NBLK, E])
        blocksum = sb("blocksum", [P, NBLK, E])
        prefix = sb("prefix", [P, NBLK + 1, E])
        iota_k = sb("iota_k", [P, E, NBLK])
        over = sb("over", [P, E, NBLK])
        tiles = sb("tiles", [P, E])
        tile_end = sb("tile_end", [P, E])
        first_slot = sb("first_slot", [P, E])
        iota_s = sb("iota_s", [P, SLOTS, E])
        ended = sb("ended", [P, SLOTS, E])
        slot_f = sb("slot_f", [P, SLOTS])
        slot_expert = sb("slot_expert", [P, SLOTS], I32)
        place = sb("place", [P, NBLK, E])
        place_hot = sb("place_hot", [P, TOPK, NBLK, E])
        pos_f = sb("pos_f", [P, TOPK, NBLK])
        pos = sb("pos", [P, TOPK, NBLK], U32)
        gap = sb("gap", [P, NBLK])
        egap = sb("egap", [P, NBLK])
        eden = sb("eden", [P, NBLK])
        wts = sb("wts", [P, TOPK, NBLK])
        zero = sb("zero", [P, DX])

        zs = [hst, hC]
        xn = u[:, :, :, :].rearrange("p q h t -> p (q h t)").rearrange("p (t d) -> p t d", t=NBLK)
        silu_g, hid, hidT, xio = dA, dBu, hst, hC
        x_tile = [xio[:, i, 0:DX] for i in range(2)]
        xT_tile = [xio[:, i, DX:2 * DX].rearrange("p (k t) -> p k t", k=2) for i in range(2)]
        y_tile = [B_rep[:, 0, i * DX:(i + 1) * DX] for i in range(2)]
        got = [zT, xn]

        bank = [stack.enter_context(nc.psum_tensor(f"bank{i}", [P, 512], F32)) for i in range(8)]
        PD, PU = bank[0:2], bank[2:4]
        PY = [bank[4:6], bank[6:8]]

        delta, du = dBu[:, 0, :], dBu[:, 1, :]
        xprojT_ps = [bank[3][:, h * 64:h * 64 + DR + 2 * DS] for h in range(2)]
        dtwT_ps = [bank[3][0:DR, (h + 1) * P:(h + 2) * P] for h in range(2)]
        A_ps = bank[3][:, 3 * P:3 * P + NG * TPG]
        cols_ps = bank[3][:, 3 * P + NG * TPG:3 * P + NG * TPG + 6]
        CONV = [bank[i][:, :] for i in (0, 1, 2, 4)]
        BCD = [[bank[5][:, :], bank[6][:, :], bank[7][0:DR, :]], [bank[0][:, :], bank[1][:, :], bank[2][0:DR, :]]]
        DRAW = [bank[i][:, :] for i in (3, 7, 4, 2)]

        x_slots = nc.dram_tensor("x_slots", [SLOTS * P, DX], F32, kind="Internal").ap()
        y_slots = nc.dram_tensor("y_slots", [SLOTS * P, DX], F32, kind="Internal").ap()

        ld = {n: sem("ld_" + n) for n in ("ctx", "inw", "convw", "small", "x", "gates", "w")}
        consts = sem("consts")
        tapw_ok, ctxT_ps, ctxT_ok, tapT_ps, tapT_ok = map(sem, ("tapw_ok", "ctxT_ps", "ctxT_ok", "tapT_ps", "tapT_ok"))
        smallT_ps, small_ok, Aexp_ok, Aneg_ok, spread_ok = map(sem, ("smallT_ps", "small_ok", "Aexp_ok", "Aneg_ok", "spread_ok"))
        tanh_ok, stats_ok, std_ok, rstd_ok, zs_ok, zT_ps, zT_ok = map(sem, ("tanh_ok", "stats_ok", "std_ok", "rstd_ok", "zs_ok", "zT_ps", "zT_ok"))
        conv_ps, u_ok, bcd_ps, bcd_ok, draw_ps, sp_act, sp_dve, delta_ok, du_ok = map(
            sem, ("conv_ps", "u_ok", "bcd_ps", "bcd_ok", "draw_ps", "sp_act", "sp_dve", "delta_ok", "du_ok"))
        dhi_ok, duhi_ok, dlo_ok, dulo_ok, skip_ps = map(sem, ("dhi_ok", "duhi_ok", "dlo_ok", "dulo_ok", "skip_ps"))
        d_spread, du_spread, exp_done, dbu_done, scan_done, hc_done, y_done = map(
            sem, ("d_spread", "du_spread", "exp_done", "dbu_done", "scan_done", "hc_done", "y_done"))
        zero_ok, zeroed = sem("zero_ok"), sem("zeroed")
        gated_ok, x2_ok, stats2_ok, std2_ok, rstd2_ok, xn_ok, xnT_ps, xnT_ok, logit_ps, logit_ok = map(
            sem, ("gated_ok", "x2_ok", "stats2_ok", "std2_ok", "rstd2_ok", "xn_ok", "xnT_ps", "xnT_ok", "logit_ps", "logit_ok"))
        route, mask_ok, rank_ps, egap_ok, slots_ok, pos_ok, scattered = map(
            sem, ("route", "mask_ok", "rank_ps", "egap_ok", "slots_ok", "pos_ok", "scattered"))
        gap_ok, cols_ok = sem("gap_ok"), sem("cols_ok")
        x_in = [sem("x_in0"), sem("x_in1")]
        xT_ps, xT_ok, g_ps, u_ps, silu_ok, hid_ok, hidT_ps, hidT_ok, y_ps, y_sb = map(
            sem, ("xT_ps", "xT_ok", "g_ps", "u_ps", "silu_ok", "hid_ok", "hidT_ps", "hidT_ok", "y_ps", "y_sb"))
        y_out = [sem("y_out0"), sem("y_out1")]
        gathered = [sem(f"gathered{i}") for i in range(NBLK)]
        comb = [sem("comb0"), sem("comb1")]
        stored = sem("stored")

        block = stack.enter_context(nc.Block())

        @block.sync
        def _(sp):
            sp.dma_start(ctx_sb, ctx_1024.rearrange("b (r p) d -> p (b r) d", p=P)).then_inc(ld["ctx"], 16)
            sp.dma_start(inw, in_proj_w.rearrange("(h p) d -> p h d", p=P)).then_inc(ld["inw"], 16)
            sp.dma_start(convw[:, :, :], conv_w.rearrange("(h p) k -> p h k", p=P)).then_inc(ld["convw"], 16)
            sp.dma_start(xs[:, :, :], x.rearrange("b (r p) d -> p (b r) d", p=P)).then_inc(ld["x"], 16)
            for e in range(E):
                sp.dma_start(W0[:, e, :, :], w0[e].rearrange("(k p) m -> p k m", p=P)).then_inc(ld["w"], 16)
                sp.dma_start(W1[:, e, :, :], w1[e].rearrange("(k p) m -> p k m", p=P)).then_inc(ld["w"], 16)
            sp.wait_ge(delta_ok, 2 * NQ)
            sp.wait_ge(conv_ps, 4)
            sp.wait_ge(spread_ok, 1)
            for e in range(E):
                sp.dma_start(WO[:, e, :, :], wo[e].rearrange("(k p) n -> p k n", p=P)).then_inc(ld["w"], 16)
            sp.wait_ge(zero_ok, 1)
            for s in range(SLOTS):
                sp.dma_start(x_slots[s * P:(s + 1) * P, :], zero[:, :]).then_inc(zeroed, 16)
            sp.wait_ge(scattered, 16 * TOPK * NBLK)

            def slot_in(s, i):
                sp.dma_start(x_tile[i], x_slots[bass.ds(s * P, P), :]).then_inc(x_in[i], 16)

            slot_in(0, 0)
            slot_in(1, 1)
            with sp.Fori(0, (SLOTS - 3) // 2) as t:
                for i in range(2):
                    sp.wait_ge(xT_ps, 2 * t + i + 1)
                    slot_in(2 * t + i + 2, i)
            sp.wait_ge(xT_ps, SLOTS - 2)
            slot_in(SLOTS - 1, (SLOTS - 1) % 2)
            for i in range(NBLK):
                sp.wait_ge(comb[1], i + 1)
                sp.dma_start(out[i // 2, (i % 2) * P:(i % 2 + 1) * P, :], xs[:, i, :]).then_inc(stored, 16)
            sp.wait_ge(stored, 16 * NBLK)

        @block.gpsimd
        def _(pool):
            pool.memset(ident[:, :], 0.0).then_inc(consts, 1)
            pool.memset(ones[:, :], 1.0).then_inc(consts, 1)
            pool.memset(spread_f, 0.0).then_inc(consts, 1)
            pool.memset(gather8[:, :], 1.0).then_inc(consts, 1)
            pool.memset(before[:, :], 1.0).then_inc(consts, 1)
            pool.memset(zero[:, :], 0.0).then_inc(zero_ok, 1)
            pool.wait_ge(consts, 5)
            pool.affine_select(out=ident[:, :], in_=ident[:, :], compare_op=ALU.not_equal, fill=1.0, base=0,
                               pattern=[[-1, P]], channel_multiplier=1).then_inc(consts, 1)
            sv = spread_f.rearrange("p (j c n) -> p j c n", j=TPG, c=CH)
            for part in range(2):
                pool.affine_select(out=sv, in_=sv, compare_op=ALU.not_equal, fill=1.0, base=-GRP * part,
                                   pattern=[[-CH, TPG], [-1, CH], [0, DS]], channel_multiplier=1).then_inc(consts, 1)
                pool.wait_ge(consts, 7 + part)
            pool.affine_select(out=gather8[:, :], in_=gather8[:, :], compare_op=ALU.is_ge, fill=0.0, base=0,
                               pattern=[[-DS, CH]], channel_multiplier=1).then_inc(consts, 1)
            pool.wait_ge(consts, 9)
            pool.affine_select(out=gather8[:, :], in_=gather8[:, :], compare_op=ALU.is_ge, fill=0.0, base=DS - 1,
                               pattern=[[DS, CH]], channel_multiplier=-1).then_inc(consts, 1)
            pool.affine_select(out=before[:, :], in_=before[:, :], compare_op=ALU.is_gt, fill=0.0, base=0,
                               pattern=[[1, P]], channel_multiplier=-1).then_inc(consts, 1)
            pool.iota(iota_e[:, :, :], pattern=[[0, NBLK], [1, E]], base=0, channel_multiplier=0,
                      allow_small_or_imprecise_dtypes=True).then_inc(consts, 1)
            pool.iota(iota_k[:, :, :], pattern=[[0, E], [P, NBLK]], base=0, channel_multiplier=0,
                      allow_small_or_imprecise_dtypes=True).then_inc(consts, 1)
            pool.iota(iota_s[:, :, :], pattern=[[1, SLOTS], [0, E]], base=0, channel_multiplier=0,
                      allow_small_or_imprecise_dtypes=True).then_inc(consts, 1)

            pool.sem_inc(hc_done, AHEAD)
            for q in range(NQ):
                pool.wait_ge(bcd_ok, 3 * q + 2)
                with pool.Fori(q * NG, (q + 1) * NG) as g:
                    for j in range(TPG):
                        n = g * TPG + j
                        pool.wait_ge(scan_done, n + 1 + AHEAD)
                        pool.wait_ge(y_done, n + 1)
                        pool.tensor_tensor(hC[:, j % 2, :], hst[:, j % 2, :], C_rep[:, q, :],
                                           ALU.mult).then_inc(hc_done, 1)

            pool.wait_ge(zeroed, 16 * SLOTS)
            pool.wait_ge(xn_ok, NBLK)
            pool.wait_ge(pos_ok, 1)
            for k in range(TOPK):
                for i in range(NBLK):
                    pool.indirect_dma_start(out=x_slots, out_offset=bass.IndirectOffsetOnAxis(ap=pos[:, k, i:i + 1], axis=0),
                                            in_=xn[:, i, :], in_offset=None).then_inc(scattered, 16)
            pool.wait_ge(scattered, 16 * TOPK * NBLK)
            for i in range(2):
                pool.wait_ge(y_out[i], 16 * ((SLOTS + 1 - i) // 2))
            for i in range(NBLK):
                for k in range(TOPK):
                    pool.indirect_dma_start(out=got[k][:, i, :], out_offset=None, in_=y_slots,
                                            in_offset=bass.IndirectOffsetOnAxis(ap=pos[:, k, i:i + 1], axis=0)).then_inc(gathered[i], 16)

        @block.scalar
        def _(act):
            for v, vec in enumerate((conv_b, dt_proj_b, D)):
                act.dma_start(vec_rows[2 * v:2 * v + 2, :], vec.rearrange("(h p) -> h p", p=P)).then_inc(ld["small"], 16)
            act.dma_start(xproj_sb[:, :], x_proj_w).then_inc(ld["small"], 16)
            act.dma_start(dtw_sb[:, :, :], dt_proj_w.rearrange("(h p) r -> p h r", p=P)).then_inc(ld["small"], 16)
            act.dma_start(Alog_sb[:, :], A_log.rearrange("(j c) n -> j (c n)", c=CH)).then_inc(ld["small"], 16)
            act.dma_start(gate_sb[:, :, :], gate_w.rearrange("(k p) e -> p k e", p=P)).then_inc(ld["small"], 16)
            for i, gv in enumerate((g_xattn, g_ffn)):
                act.dma_start(gates[:, i:i + 1], gv.rearrange("(a n) -> a n", a=1).to_broadcast((P, 1))).then_inc(ld["gates"], 16)
            act.wait_ge(ld["gates"], 32)
            act.activation(tg[:, :], gates[:, :], ACT.Tanh).then_inc(tanh_ok, 1)
            for h in range(2):
                act.wait_ge(tapT_ps, h + 1)
                act.activation(tapwT[:, h, :, :].rearrange("p k e -> p (k e)"), bank[6 + h][:, :], ACT.Copy).then_inc(tapT_ok, 1)
            act.wait_ge(stats_ok, NBLK * 2 + 1)
            act.activation(std[:, 0, :], vare[:, 0, :], ACT.Sqrt).then_inc(std_ok, 1)
            act.wait_ge(rstd_ok, 2)
            for i in range(NBLK):
                q, r = divmod(i, QBLK)
                act.activation(zs[q][:, r // 2, (r % 2) * DX:(r % 2 + 1) * DX], xs[:, i, :], ACT.Silu,
                               bias=nmr[:, i:i + 1], scale=rstd[:, 0, i:i + 1]).then_inc(zs_ok, 1)
            act.wait_ge(cols_ok, 1)
            for q in range(NQ):
                for h in range(2):
                    act.wait_ge(conv_ps, 2 * q + h + 1)
                    act.activation(u[:, q, h, :], CONV[2 * q + h], ACT.Silu, bias=cols[:, 0, h:h + 1]).then_inc(u_ok, 1)
            act.wait_ge(smallT_ps, 1)
            act.activation(Aexp[:, :], A_ps, ACT.Exp).then_inc(Aexp_ok, 1)
            for q in range(NQ):
                for h in range(2):
                    c = 2 * q + h
                    act.wait_ge(draw_ps, c + 1)
                    if c:
                        act.wait_ge(delta_ok, c)
                    act.activation(sp_relu, DRAW[c], ACT.Relu, bias=cols[:, 1, h:h + 1]).then_inc(sp_act, 1)
                    act.activation(sp_exp, DRAW[c], ACT.Abs, bias=cols[:, 1, h:h + 1]).then_inc(sp_act, 1)
                    act.wait_ge(sp_act, 4 * c + 2)
                    act.activation(sp_exp, sp_exp, ACT.Exp, scale=-1.0).then_inc(sp_act, 1)
                    act.wait_ge(sp_act, 4 * c + 3)
                    act.activation(sp_ln, sp_exp, ACT.Ln, bias=1.0).then_inc(sp_act, 1)
                    for parts, src, ready, done in ((d_parts, delta, delta_ok, dhi_ok), (du_parts, du, du_ok, duhi_ok)):
                        act.wait_ge(ready, c + 1)
                        for k in range(2):
                            rows = slice(GRP * k, GRP * (k + 1))
                            act.activation(parts[rows, q * NG + 2 * h + k, :], src[rows, :], ACT.Copy).then_inc(done, 1)
            act.wait_ge(Aneg_ok, 1)
            act.sem_inc(exp_done, AHEAD)
            for q in range(NQ):
                with act.Fori(q * NG, (q + 1) * NG) as g:
                    for j in range(TPG):
                        n = g * TPG + j
                        act.wait_ge(d_spread, n + 1)
                        act.wait_ge(scan_done, n + 1)
                        act.activation(dA[:, j % 2, :].rearrange("p (b l) -> p b l", b=QB)[:, :, 1:L],
                                       PD[j % 2][:, :].rearrange("p (b l) -> p b l", b=QB)[:, :, 1:L],
                                       ACT.Exp, scale=Aneg[:, bass.ds(n, 1)]).then_inc(exp_done, 1)
            for q in range(NQ):
                act.wait_ge(stats2_ok, (q + 1) * (2 * QBLK + 1))
                act.activation(std[:, 1, q * QBLK:(q + 1) * QBLK], vare[:, 1, q * QBLK:(q + 1) * QBLK], ACT.Sqrt).then_inc(std2_ok, 1)
            act.wait_ge(gap_ok, 1)
            act.activation(egap[:, :], gap[:, :], ACT.Exp).then_inc(egap_ok, 1)

            act.wait_ge(scattered, 16 * TOPK * NBLK)

            def xT_out(s, i):
                act.wait_ge(xT_ps, s + 1)
                if not (isinstance(s, int) and s < 2):
                    act.wait_ge(u_ps, s - 1)
                act.activation(xT_tile[i].rearrange("p k t -> p (k t)"), bank[6][:, i * DX:(i + 1) * DX], ACT.Copy).then_inc(xT_ok, 1)

            def silu(s, i):
                act.wait_ge(g_ps, s + 1)
                if not (isinstance(s, int) and s < 2):
                    act.wait_ge(hid_ok, s - 1)
                act.activation(silu_g[:, i, :], bank[i][:, :], ACT.Silu).then_inc(silu_ok, 1)

            def y_store(s, i, reused):
                act.wait_ge(y_ps, s + 1)
                if reused is not None:
                    act.wait_ge(y_out[i], reused)
                act.activation(y_tile[i], bank[7][:, i * DX:(i + 1) * DX], ACT.Copy).then_inc(y_sb, 1)
                act.wait_ge(y_sb, s + 1)
                act.dma_start(y_slots[bass.ds(s * P, P), :], y_tile[i]).then_inc(y_out[i], 16)

            xT_out(0, 0)
            xT_out(1, 1)
            silu(0, 0)
            for s in range(2):
                xT_out(s + 2, s)
                silu(s + 1, (s + 1) % 2)
                y_store(s, s, None)
            with act.Fori(1, (SLOTS - 3) // 2) as t:
                for i in range(2):
                    xT_out(2 * t + i + 2, i)
                    silu(2 * t + i + 1, (i + 1) % 2)
                    y_store(2 * t + i, i, 16 * t)
            for s in range(SLOTS - 3, SLOTS):
                if s + 2 < SLOTS:
                    xT_out(s + 2, s % 2)
                if s + 1 < SLOTS:
                    silu(s + 1, (s + 1) % 2)
                y_store(s, s % 2, 16 * (s // 2))

        @block.tensor
        def _(pe):
            pe.wait_ge(consts, 14)
            pe.wait_ge(ld["ctx"], 16)
            for t in range(NBLK):
                pe.transpose(bank[4 + t // 4][:, (t % 4) * P:(t % 4 + 1) * P], ctx_sb[:, t, :], ident[:, :]).then_inc(ctxT_ps, 1)
            for h in range(2):
                pe.wait_ge(tapw_ok, DC * (h + 1))
                for k in range(DC):
                    mm = pe.transpose(bank[6 + h][:, k * P:(k + 1) * P], tapw[:, h, k, :], ident[:, :])
                mm.then_inc(tapT_ps, 1)
            pe.wait_ge(ld["small"], 16 * 7)
            for h in range(2):
                pe.transpose(xprojT_ps[h], xproj_sb[:, h * P:(h + 1) * P], ident[0:DR + 2 * DS, 0:DR + 2 * DS])
                pe.transpose(dtwT_ps[h], dtw_sb[:, h, :], ident[:, :])
            pe.transpose(cols_ps, vec_rows[:, :], ident[0:6, 0:6])
            pe.transpose(A_ps, Alog_sb[:, :], ident[0:NG * TPG, 0:NG * TPG]).then_inc(smallT_ps, 1)
            pe.wait_ge(ctxT_ok, 3)
            for q in range(NQ):
                for h in range(2):
                    pe.wait_ge(tapT_ok, h + 1)
                    for k in range(DC):
                        mm = pe.matmul(CONV[2 * q + h].rearrange("p (b l) -> p b l", b=QB), tapwT[:, h, k, :],
                                       ctxT[:, q * QB:(q + 1) * QB, k:k + L], start=(k == 0), stop=(k == DC - 1))
                    mm.then_inc(conv_ps, 1)
            pe.wait_ge(small_ok, 5)
            pe.wait_ge(Aexp_ok, 1)
            for q in range(NQ):
                pe.wait_ge(u_ok, 2 * q + 2)
                pe.wait_ge(tapT_ok, 2)
                for n, w in enumerate((xprojT_B, xprojT_C, xprojT_dt)):
                    for h in range(2):
                        lhsT = w[:, h, :] if n == 2 else w[:, h, :, :].rearrange("p c n -> p (c n)")
                        mm = pe.matmul(BCD[q][n], lhsT, u[:, q, h, :], start=(h == 0), stop=(h == 1))
                    mm.then_inc(bcd_ps, 1)
                pe.wait_ge(bcd_ok, 3 * q + 3)
                for h in range(2):
                    pe.matmul(DRAW[2 * q + h], dtwT[:, h, :], dt_lo[:, q, :], start=True, stop=True).then_inc(draw_ps, 1)
            pe.wait_ge(small_ok, 7)
            for b in range(B):
                q, r = divmod(b, QB)
                pe.wait_ge(zs_ok, 2 * b + 2)
                if b == 0:
                    pe.wait_ge(sp_act, 16)
                    pe.wait_ge(bcd_ok, 6)
                for l in range(2):
                    for h in range(2):
                        mm = pe.transpose(bank[4 + b][:, l * DX + h * P:l * DX + (h + 1) * P],
                                          zs[q][:, r, h * DX + l * P:h * DX + (l + 1) * P], ident[:, :])
                mm.then_inc(zT_ps, 1)
            for b in range(B):
                q, r = divmod(b, QB)
                pe.wait_ge(zT_ok, b + 1)
                for l in range(2):
                    for h in range(2):
                        pe.matmul(PY[q][r][:, l * DX + h * P:l * DX + (h + 1) * P],
                                  u[:, q, h, r * L + l * P:r * L + (l + 1) * P], diagD[:, h, :],
                                  start=(l == 0 and h == 0), stop=False, skip_group_check=True).then_inc(skip_ps, 1)

            def spread_tile(g, j, n):
                pe.wait_ge(exp_done, n + 1)
                pe.matmul(PD[j % 2][:, :], spread[:, j, :], d_parts[:, bass.ds(g, 1), :].rearrange("p o t -> p (o t)"),
                          start=True, stop=True).then_inc(d_spread, 1)
                pe.wait_ge(dbu_done, n + 1)
                pe.matmul(PU[j % 2][:, :], spread[:, j, :], du_parts[:, bass.ds(g, 1), :].rearrange("p o t -> p (o t)"),
                          start=True, stop=True).then_inc(du_spread, 1)

            def sum_states(q, g, j, n):
                pe.wait_ge(hc_done, n + 1 + AHEAD)
                for k in range(QBLK):
                    at = (k % 2) * DX + (g - q * NG) * GRP + j * CH
                    mm = pe.matmul(PY[q][k // 2][:, bass.ds(at, CH)], hC[:, j % 2, k * P:(k + 1) * P], gather8[:, :],
                                   start=False, stop=False, skip_group_check=True)
                mm.then_inc(y_done, 1)

            def group(q, g, last):
                for j in range(TPG):
                    n = g * TPG + j
                    if j + 2 < TPG:
                        spread_tile(g, j + 2, n + 2)
                    elif not last:
                        spread_tile(g + 1, j + 2 - TPG, n + 2)
                    sum_states(q, g, j, n)

            pe.wait_ge(dlo_ok, 2 * NQ * 2)
            pe.wait_ge(dulo_ok, 2 * NQ * 2)
            pe.wait_ge(dhi_ok, 2 * NQ * 2)
            pe.wait_ge(duhi_ok, 2 * NQ * 2)
            pe.wait_ge(spread_ok, 1)
            pe.sem_inc(y_done, AHEAD)
            spread_tile(0, 0, 0)
            spread_tile(0, 1, 1)
            with pe.Fori(0, NG) as g:
                group(0, g, False)
            with pe.Fori(NG, 2 * NG - 1) as g:
                group(1, g, False)
            group(1, 2 * NG - 1, True)

            pe.wait_ge(ld["small"], 16 * 7)
            for q in range(NQ):
                pe.wait_ge(gated_ok, 2 * q + 2)
                pe.wait_ge(xn_ok, (q + 1) * QBLK)
                for i in range(QBLK):
                    for k in range(2):
                        mm = pe.transpose(PY[q][i // 2][:, (i % 2) * DX + k * P:(i % 2) * DX + (k + 1) * P],
                                          xn[:, q * QBLK + i, k * P:(k + 1) * P], ident[:, :])
                    if i % 2:
                        mm.then_inc(xnT_ps, 1)
                pe.wait_ge(xnT_ok, 2 * q + 2)
                for i in range(QBLK):
                    for k in range(2):
                        mm = pe.matmul(PY[q][0][:, i * E:(i + 1) * E], xnT[:, i, k, :], gate_sb[:, k, :],
                                       start=(k == 0), stop=(k == 1))
                mm.then_inc(logit_ps, 1)
            pe.wait_ge(mask_ok, 1)
            m = mask[:, :, :].rearrange("p t e -> p (t e)")
            pe.matmul(bank[0][:, 0:NBLK * E], before[:, :], m, start=True, stop=True)
            pe.matmul(bank[1][:, 0:NBLK * E], ones[:, :], m, start=True, stop=True).then_inc(rank_ps, 1)

            pe.wait_ge(slots_ok, 1)
            pe.wait_ge(ld["w"], 16 * 3 * E)

            def x_turn(s, i, loaded):
                pe.wait_ge(x_in[i], loaded)
                if not (isinstance(s, int) and s < 1):
                    pe.wait_ge(xT_ok, s)
                for k in range(2):
                    mm = pe.transpose(bank[6][:, i * DX + k * P:i * DX + (k + 1) * P], x_tile[i][:, k * P:(k + 1) * P], ident[:, :])
                mm.then_inc(xT_ps, 1)

            def product(W, dest, i, expert, done):
                for k in range(2):
                    mm = pe.matmul(dest[i][:, :], xT_tile[i][:, k, :], W[:, bass.ds(expert, 1), k, :].rearrange("p o m -> p (o m)"),
                                   start=(k == 0), stop=(k == 1))
                mm.then_inc(done, 1)

            def gate(s, i, expert):
                pe.wait_ge(xT_ok, s + 1)
                if not (isinstance(s, int) and s < 2):
                    pe.wait_ge(silu_ok, s - 1)
                product(W0, bank[0:2], i, expert, g_ps)

            def up(s, i, expert):
                if not (isinstance(s, int) and s < 2):
                    pe.wait_ge(hid_ok, s - 1)
                product(W1, bank[2:4], i, expert, u_ps)

            def hid_turn(s, i):
                pe.wait_ge(hid_ok, s + 1)
                if not (isinstance(s, int) and s < 2):
                    pe.wait_ge(hidT_ok, s - 1)
                for k in range(4):
                    mm = pe.transpose(bank[4 + i][:, k * P:(k + 1) * P], hid[:, i, k * P:(k + 1) * P], ident[:, :])
                mm.then_inc(hidT_ps, 1)

            def down(s, i, expert):
                pe.wait_ge(hidT_ok, s + 1)
                if not (isinstance(s, int) and s < 1):
                    pe.wait_ge(y_sb, s)
                for k in range(4):
                    mm = pe.matmul(bank[7][:, i * DX:(i + 1) * DX], hidT[:, i, k * P:(k + 1) * P],
                                   WO[:, bass.ds(expert, 1), k, :].rearrange("p o n -> p (o n)"), start=(k == 0), stop=(k == 3))
                mm.then_inc(y_ps, 1)

            def expert_of(s):
                return pe.value_load(slot_expert[0:1, bass.ds(s, 1)], min_val=0, max_val=E - 1)

            def step(s, i, loaded, turn=True, nxt=True):
                now = expert_of(s)
                if turn:
                    x_turn(s + 2, i, loaded)
                if nxt:
                    follows = expert_of(s + 1)
                    gate(s + 1, 1 - i, follows)
                hid_turn(s, i)
                if nxt:
                    up(s + 1, 1 - i, follows)
                down(s, i, now)

            x_turn(0, 0, 16)
            x_turn(1, 1, 16)
            first = expert_of(0)
            gate(0, 0, first)
            up(0, 0, first)
            step(0, 0, 32)
            step(1, 1, 32)
            with pe.Fori(1, (SLOTS - 3) // 2) as t:
                for i in range(2):
                    step(2 * t + i, i, 16 * t + 32)
            step(SLOTS - 3, 0, 16 * ((SLOTS + 1) // 2))
            step(SLOTS - 2, 1, 0, turn=False)
            step(SLOTS - 1, 0, 0, turn=False, nxt=False)

        @block.vector
        def _(dve):
            dve.memset(dA[:, :, :], 0.0).then_inc(scan_done, AHEAD)
            dve.memset(ctxT[:, :, 0:DC - 1], 0.0).then_inc(ctxT_ok, 1)
            dve.wait_ge(ld["inw"], 16)
            dve.wait_ge(ld["convw"], 16)
            for h in range(2):
                for k in range(DC):
                    dve.tensor_scalar(tapw[:, h, k, :], inw[:, h, :], convw[:, h, k:k + 1], None, ALU.mult).then_inc(tapw_ok, 1)
            for q in range(NQ):
                dve.wait_ge(ctxT_ps, 4 * (q + 1))
                dve.tensor_copy(ctxT[:, q * QB:(q + 1) * QB, DC - 1:], bank[4 + q][:, :].rearrange("p (b l) -> p b l", b=QB)).then_inc(ctxT_ok, 1)
            dve.wait_ge(smallT_ps, 1)
            dve.tensor_copy(cols[:, :, :].rearrange("p v h -> p (v h)"), cols_ps).then_inc(cols_ok, 1)
            for h in range(2):
                dve.tensor_copy(xprojT_dt[:, h, :], xprojT_ps[h][:, 0:DR])
                for n, w in enumerate((xprojT_B, xprojT_C)):
                    src = xprojT_ps[h][:, DR + n * DS:DR + (n + 1) * DS].rearrange("p (o n) -> p o n", o=1).to_broadcast((P, CH, DS))
                    dve.tensor_copy(w[:, h, :, :], src).then_inc(small_ok, 1)
            dve.tensor_copy(dtwT[:, :, :].rearrange("r h e -> r (h e)"), bank[3][0:DR, P:3 * P]).then_inc(small_ok, 1)
            dve.wait_ge(ld["x"], 16)
            for i in range(NBLK):
                dve.bn_stats(stats[:, 0, i, :], xs[:, i, :]).then_inc(stats_ok, 1)
            for i in range(NBLK):
                dve.wait_ge(stats_ok, NBLK + i)
                dve.bn_aggr(mv[:, 0, i, :], stats[:, 0, i, :]).then_inc(stats_ok, 1)
            dve.wait_ge(stats_ok, 2 * NBLK)
            dve.tensor_scalar(vare[:, 0, :], mv[:, 0, :, 1], EPS, None, ALU.add).then_inc(stats_ok, 1)
            dve.wait_ge(std_ok, 1)
            dve.reciprocal(rstd[:, 0, :], std[:, 0, :]).then_inc(rstd_ok, 1)
            dve.wait_ge(rstd_ok, 1)
            dve.scalar_tensor_tensor(out=nmr[:, :], in0=mv[:, 0, :, 0], scalar=-1.0, in1=rstd[:, 0, :],
                                     op0=ALU.mult, op1=ALU.mult).then_inc(rstd_ok, 1)
            dve.wait_ge(consts, 14)
            dve.tensor_copy(spread[:, :, :].rearrange("p j m -> p (j m)"), spread_f).then_inc(spread_ok, 1)
            dve.wait_ge(cols_ok, 1)
            for h in range(2):
                dve.tensor_scalar(diagD[:, h, :], ident[:, :], cols[:, 2, h:h + 1], None, ALU.mult).then_inc(small_ok, 1)

            for q in range(NQ):
                for n, dst in enumerate((B_rep[:, q, :], C_rep[:, q, :], dt_lo[:, q, :])):
                    dve.wait_ge(bcd_ps, 3 * q + n + 1)
                    dve.tensor_copy(dst, BCD[q][n]).then_inc(bcd_ok, 1)
                if q == 0:
                    dve.wait_ge(Aexp_ok, 1)
                    for k in range(NQ):
                        dve.tensor_scalar(Aneg[:, k * NG * TPG:(k + 1) * NG * TPG], Aexp[:, :], -1.0, None, ALU.mult).then_inc(Aneg_ok, 1)
                for h in range(2):
                    c = 2 * q + h
                    dve.wait_ge(sp_act, 4 * c + 3)
                    dve.tensor_scalar(sp_rest, sp_exp, 1.0, None, ALU.add).then_inc(sp_dve, 1)
                    dve.wait_ge(sp_dve, 3 * c + 1)
                    dve.scalar_tensor_tensor(out=sp_rest, in0=sp_rest, scalar=1.0, in1=sp_exp,
                                             op0=ALU.subtract, op1=ALU.subtract).then_inc(sp_dve, 1)
                    dve.wait_ge(sp_act, 4 * c + 4)
                    dve.wait_ge(sp_dve, 3 * c + 2)
                    dve.tensor_tensor(sp_rest, sp_ln, sp_rest, ALU.subtract).then_inc(sp_dve, 1)
                    dve.wait_ge(sp_dve, 3 * c + 3)
                    if c:
                        dve.wait_ge(dhi_ok, 2 * c)
                        dve.wait_ge(duhi_ok, 2 * c)
                    dve.tensor_tensor(delta, sp_rest, sp_relu, ALU.add).then_inc(delta_ok, 1)
                    dve.wait_ge(delta_ok, c + 1)
                    dve.tensor_tensor(du, delta, u[:, q, h, :], ALU.mult).then_inc(du_ok, 1)
                    dve.wait_ge(du_ok, c + 1)
                    for parts, src, ready, done in ((d_parts, delta, dhi_ok, dlo_ok), (du_parts, du, duhi_ok, dulo_ok)):
                        for k in range(2):
                            rows, other = slice(GRP * k, GRP * (k + 1)), slice(GRP * (1 - k), GRP * (2 - k))
                            dve.wait_ge(ready, 2 * c + k + 1)
                            dve.tensor_tensor(parts[other, q * NG + 2 * h + k, :], src[rows, :],
                                              parts[rows, q * NG + 2 * h + k, :], ALU.subtract).then_inc(done, 1)
            dve.wait_ge(tanh_ok, 1)
            for b in range(B):
                dve.wait_ge(zT_ps, b + 1)
                dve.tensor_scalar(zT[:, 2 * b:2 * b + 2, :].rearrange("p t d -> p (t d)"), bank[4 + b][:, :],
                                  tg[:, 0:1], None, ALU.mult).then_inc(zT_ok, 1)

            def drive(q, j, n):
                dve.wait_ge(du_spread, n + 1)
                dve.wait_ge(scan_done, n + 1)
                dve.tensor_tensor(dBu[:, j % 2, :], PU[j % 2][:, :], B_rep[:, q, :], ALU.mult).then_inc(dbu_done, 1)

            def scan(j, n):
                dve.wait_ge(exp_done, n + 1 + AHEAD)
                dve.wait_ge(dbu_done, n + 1 + AHEAD)
                dve.wait_ge(hc_done, n + 1)
                dve.tensor_tensor_scan(hst[:, j % 2, :], dA[:, j % 2, :], dBu[:, j % 2, :], 0.0,
                                       ALU.mult, ALU.add).then_inc(scan_done, 1)

            def group(q, g, after):
                for j in range(TPG):
                    n = g * TPG + j
                    if j + 1 < TPG:
                        drive(q, j + 1, n + 1)
                    elif after is not None:
                        drive(after, 0, n + 1)
                    scan(j, n)

            dve.wait_ge(zT_ps, B)
            dve.sem_inc(dbu_done, AHEAD)
            drive(0, 0, 0)
            with dve.Fori(0, NG - 1) as g:
                group(0, g, 0)
            group(0, NG - 1, 1)
            with dve.Fori(NG, 2 * NG - 1) as g:
                group(1, g, 1)
            group(1, 2 * NG - 1, None)

            for q in range(NQ):
                dve.wait_ge(y_done, AHEAD + (q + 1) * NG * TPG)
                for r in range(QB):
                    b = q * QB + r
                    zb = zT[:, 2 * b:2 * b + 2, :].rearrange("p t d -> p (t d)")
                    xb = xs[:, 2 * b:2 * b + 2, :].rearrange("p t d -> p (t d)")
                    dve.tensor_tensor(zb, PY[q][r][:, :], zb, ALU.mult).then_inc(gated_ok, 1)
                    dve.wait_ge(gated_ok, b + 1)
                    dve.tensor_tensor(xb, zb, xb, ALU.add).then_inc(x2_ok, 1)
                base = q * (2 * QBLK + 1)
                for r in range(QBLK):
                    dve.wait_ge(x2_ok, q * QB + r // 2 + 1)
                    dve.bn_stats(stats[:, 1, q * QBLK + r, :], xs[:, q * QBLK + r, :]).then_inc(stats2_ok, 1)
                for r in range(QBLK):
                    dve.wait_ge(stats2_ok, base + QBLK + r)
                    dve.bn_aggr(mv[:, 1, q * QBLK + r, :], stats[:, 1, q * QBLK + r, :]).then_inc(stats2_ok, 1)
                dve.wait_ge(stats2_ok, base + 2 * QBLK)
                cut = slice(q * QBLK, (q + 1) * QBLK)
                dve.tensor_scalar(vare[:, 1, cut], mv[:, 1, cut, 1], EPS, None, ALU.add).then_inc(stats2_ok, 1)
                dve.wait_ge(std2_ok, q + 1)
                dve.reciprocal(rstd[:, 1, cut], std[:, 1, cut]).then_inc(rstd2_ok, 1)
                dve.wait_ge(rstd2_ok, q + 1)
                for r in range(QBLK):
                    i = q * QBLK + r
                    dve.tensor_scalar(xn[:, i, :], xs[:, i, :], mv[:, 1, i, 0:1], rstd[:, 1, i:i + 1],
                                      ALU.subtract, ALU.mult).then_inc(xn_ok, 1)
                for r in range(2):
                    dve.wait_ge(xnT_ps, 2 * q + r + 1)
                    if q:
                        dve.wait_ge(logit_ps, 1)
                    dve.tensor_copy(xnT[:, 2 * r:2 * r + 2, :, :].rearrange("p t k n -> p (t k n)"), PY[q][r][:, :]).then_inc(xnT_ok, 1)
                dve.wait_ge(logit_ps, q + 1)
                dve.tensor_copy(logits[:, cut, :].rearrange("p t e -> p (t e)"), PY[q][0][:, 0:QBLK * E]).then_inc(logit_ok, 1)
                dve.wait_ge(logit_ok, q + 1)
                for r in range(QBLK):
                    i = q * QBLK + r
                    dve.max(top[:, i, :], logits[:, i, :]).then_inc(route, 1)
                for r in range(QBLK):
                    i = q * QBLK + r
                    dve.wait_ge(route, q * 2 * QBLK + QBLK + r)
                    dve.max_index(topi[:, i, :], top[:, i, :], logits[:, i, :]).then_inc(route, 1)

            steps = [2 * NBLK]

            def link(ins):
                ins.then_inc(route, 1)
                steps[0] += 1
                dve.wait_ge(route, steps[0])

            dve.wait_ge(route, steps[0])
            dve.tensor_tensor(gap[:, :], top[:, :, 1], top[:, :, 0], ALU.subtract).then_inc(gap_ok, 1)
            link(dve.tensor_copy(topf[:, :, :], topi[:, :, 0:TOPK].rearrange("p t k -> p k t")))
            for k in range(TOPK):
                link(dve.tensor_tensor(hot[:, k, :, :], iota_e[:, :, :],
                                       topf[:, k, :].rearrange("p (t o) -> p t o", o=1).to_broadcast((P, NBLK, E)), ALU.is_equal))
            dve.tensor_tensor(mask[:, :, :], hot[:, 0, :, :], hot[:, 1, :, :], ALU.add).then_inc(mask_ok, 1)
            dve.wait_ge(rank_ps, 1)
            dve.tensor_copy(rank[:, :, :].rearrange("p t e -> p (t e)"), bank[0][:, 0:NBLK * E])
            link(dve.tensor_copy(blocksum[:, :, :].rearrange("p t e -> p (t e)"), bank[1][:, 0:NBLK * E]))
            link(dve.memset(prefix[:, 0, :], 0.0))
            for i in range(NBLK):
                link(dve.tensor_tensor(prefix[:, i + 1, :], prefix[:, i, :], blocksum[:, i, :], ALU.add))
            count = prefix[:, NBLK, :].rearrange("p (e o) -> p e o", o=1).to_broadcast((P, E, NBLK))
            link(dve.tensor_tensor(over[:, :, :], count, iota_k[:, :, :], ALU.is_gt))
            link(dve.tensor_reduce(tiles[:, :], over[:, :, :], AX_X, ALU.add))
            link(dve.tensor_tensor_scan(tile_end[:, :], ones[:, 0:E], tiles[:, :], 0.0, ALU.mult, ALU.add))
            link(dve.tensor_tensor(first_slot[:, :], tile_end[:, :], tiles[:, :], ALU.subtract))
            ends = tile_end[:, :].rearrange("p (o e) -> p o e", o=1).to_broadcast((P, SLOTS, E))
            link(dve.tensor_tensor(ended[:, :, :], iota_s[:, :, :], ends, ALU.is_ge))
            link(dve.tensor_reduce(slot_f[:, :], ended[:, :, :], AX_X, ALU.add))
            dve.tensor_scalar(slot_expert[:, :], slot_f[:, :], float(E - 1), None, ALU.min).then_inc(slots_ok, 1)
            link(dve.tensor_scalar(first_slot[:, :], first_slot[:, :], float(P), None, ALU.mult))
            link(dve.tensor_tensor(place[:, :, :], rank[:, :, :], prefix[:, 0:NBLK, :], ALU.add))
            link(dve.tensor_tensor(place[:, :, :], place[:, :, :],
                                   first_slot[:, :].rearrange("p (o e) -> p o e", o=1).to_broadcast((P, NBLK, E)), ALU.add))
            for k in range(TOPK):
                link(dve.tensor_tensor(place_hot[:, k, :, :], hot[:, k, :, :], place[:, :, :], ALU.mult))
            link(dve.tensor_reduce(pos_f[:, :, :].rearrange("p k t -> p (k t)"),
                                   place_hot[:, :, :, :].rearrange("p k t e -> p (k t) e"), AX_X, ALU.add))
            dve.tensor_copy(pos[:, :, :], pos_f[:, :, :]).then_inc(pos_ok, 1)
            dve.wait_ge(egap_ok, 1)
            link(dve.tensor_scalar(eden[:, :], egap[:, :], 1.0, None, ALU.add))
            link(dve.reciprocal(eden[:, :], eden[:, :]))
            link(dve.tensor_scalar(wts[:, 0, :], eden[:, :], tg[:, 1:2], None, ALU.mult))
            link(dve.tensor_tensor(wts[:, 1, :], wts[:, 0, :], egap[:, :], ALU.mult))

            def hidden(s, i, used):
                dve.wait_ge(silu_ok, s + 1)
                dve.wait_ge(u_ps, s + 1)
                if used is not None:
                    dve.wait_ge(hidT_ps, used)
                dve.tensor_tensor(hid[:, i, :], bank[2 + i][:, :], silu_g[:, i, :], ALU.mult).then_inc(hid_ok, 1)

            def turned(s, i, used):
                dve.wait_ge(hidT_ps, s + 1)
                if used is not None:
                    dve.wait_ge(y_ps, used)
                dve.tensor_copy(hidT[:, i, :], bank[4 + i][:, :]).then_inc(hidT_ok, 1)

            for s in range(2):
                hidden(s, s, None)
                turned(s, s, None)
            with dve.Fori(1, (SLOTS - 1) // 2) as t:
                for i in range(2):
                    hidden(2 * t + i, i, 2 * t + i - 1)
                    turned(2 * t + i, i, 2 * t + i - 1)
            hidden(SLOTS - 1, 0, SLOTS - 2)
            turned(SLOTS - 1, 0, SLOTS - 2)

            for i in range(NBLK):
                dve.wait_ge(gathered[i], 16 * TOPK)
                for k in range(TOPK):
                    dve.scalar_tensor_tensor(out=xs[:, i, :], in0=got[k][:, i, :], scalar=wts[:, k, i:i + 1],
                                             in1=xs[:, i, :], op0=ALU.mult, op1=ALU.add).then_inc(comb[k], 1)
                    if k == 0:
                        dve.wait_ge(comb[0], i + 1)


INPUTS = ("x", "ctx_1024", "g_xattn", "g_ffn", "L0_xattn_in_proj_w", "L0_xattn_conv_w", "L0_xattn_conv_b",
          "L0_xattn_x_proj_w", "L0_xattn_dt_proj_w", "L0_xattn_dt_proj_b", "L0_xattn_A_log", "L0_xattn_D",
          "L0_ffn_gate_w", "L0_ffn_w0", "L0_ffn_w1", "L0_ffn_wo")


def kernel(**inputs):
    import concourse.bacc as bacc
    from concourse.bass_utils import run_bass_kernel_spmd

    nc = bacc.Bacc("TRN2", target_bir_lowering=False, num_devices=1)
    arrays, args = {}, []
    for name in INPUTS:
        a = np.ascontiguousarray(inputs[name])
        arrays["in_" + name] = a
        args.append(nc.dram_tensor("in_" + name, a.shape, mybir.dt.from_np(a.dtype), kind="ExternalInput").ap())
    out = nc.dram_tensor("out", (B, L, DX), F32, kind="ExternalOutput").ap()
    build(nc, *args, out)
    result = run_bass_kernel_spmd(nc, [arrays], core_ids=[0])
    return result.results[0]["out"]
```

```python
from contextlib import ExitStack

import numpy as np

import concourse.bass as bass
from concourse import mybir

F32 = mybir.dt.float32
F32R = mybir.dt.float32r
I32 = mybir.dt.int32
U32 = mybir.dt.uint32
ALU = mybir.AluOpType
ACT = mybir.ActivationFunctionType
AX_X = mybir.AxisListType.X

P = 128
B, L, DX = 4, 256, 256
DM, DI, DS, DC, DR = 128, 256, 16, 4, 8
E, MH, TOPK = 8, 512, 2
TOK = B * L
NBLK = TOK // P
NQ = 2
QB = B // NQ
QT = QB * L
QBLK = QT // P
CH = P // DS
GRP = 64
NG = DI // GRP
TPG = GRP // CH
TPH = 2 * TPG
SLOTS = (TOK * TOPK - E) // P + E
EPS = 1e-5
PE_POST = (5, 14, 3, 7, 11)
GATE_AT = (20, 36, 52)
RESIDUAL_AT, NORM_AT, XNT_AT, LGT_AT, BEST_AT, PLACE_AT = 40, 46, 50, 54, 58, 62
ROOT_AT = 42
LEAD = 4
AHEAD = 2


def build(nc, x, ctx_1024, g_xattn, g_ffn, in_proj_w, conv_w, conv_b, x_proj_w, dt_proj_w, dt_proj_b,
          A_log, D, gate_w, w0, w1, wo, out):
    stack = ExitStack()
    with stack:
        def sb(name, shape, dt=F32):
            return stack.enter_context(nc.sbuf_tensor(name, shape, dt))

        def sem(name):
            return stack.enter_context(nc.semaphore(name))

        W0 = sb("W0", [P, E, 2, MH])
        W1 = sb("W1", [P, E, 2, MH])
        WO = sb("WO", [P, E, 4, DX])
        early = WO[:, :, :, :].rearrange("p e k n -> p (e k n)")
        taken = [0]

        def early_part(n):
            taken[0] += n
            return early[:, taken[0] - n:taken[0]]

        ctx_sb = early_part(NBLK * DM).rearrange("p (t d) -> p t d", t=NBLK)
        ctxT = early_part(B * (L + DC - 1)).rearrange("p (b l) -> p b l", b=B)
        tapw = early_part(2 * DC * DM).rearrange("p (h k d) -> p h k d", h=2, k=DC)
        tapwT = early_part(2 * DC * P).rearrange("p (h k e) -> p h k e", h=2, k=DC)
        sp_relu, sp_ln, sp_rest = ([early_part(QT) for h in range(2)] for _ in range(3))
        inw = early_part(2 * DM).rearrange("p (h d) -> p h d", h=2)
        assert taken[0] <= E * 4 * DX

        d_parts = sb("d_parts", [P, NQ * NG, QT], F32R)
        du_parts = sb("du_parts", [P, NQ * NG, QT], F32R)
        B_rep = sb("B_rep", [P, NQ, QT])
        C_rep = sb("C_rep", [P, NQ, QT])
        dA = sb("dA", [P, 2, QT])
        dBu = sb("dBu", [P, 2, QT])
        hst = sb("hst", [P, 2, QT])
        hC = sb("hC", [P, 2, QT])
        u = sb("u", [P, NQ, 2, QT])
        xs = sb("xs", [P, NBLK, DX])
        zs = sb("zs", [P, NBLK, DX])
        spread = sb("spread", [P, TPG, P], F32R)
        sum16 = sb("sum16", [P, TPH, P])
        ident = sb("ident", [P, P])
        ones = sb("ones", [P, P])
        before = sb("before", [P, P])
        Aneg = sb("Aneg", [P, NQ * NG * TPG])
        Aexp = sb("Aexp", [P, NG * TPG])
        Alog_sb = sb("Alog_sb", [NG * TPG, P])
        zero = sb("zero", [P, DX])
        xproj_sb = zero[0:DR + 2 * DS, :]
        xprojT_B = sb("xprojT_B", [P, 2, CH, DS])
        xprojT_C = sb("xprojT_C", [P, 2, CH, DS])
        xprojT_dt = sb("xprojT_dt", [P, 2, DR])
        dtw_sb = sb("dtw_sb", [P, 2, DR])
        dtwT = sb("dtwT", [DR, 2, P])
        convw = sb("convw", [P, 2, DC])
        cols = sb("cols", [P, 3, 2])
        vec_rows = sb("vec_rows", [6, P])
        gates = sb("gates", [P, 2])
        tg = sb("tg", [P, 2])
        stats = sb("stats", [P, 2, NBLK, 6])
        mv = sb("mv", [P, 2, NBLK, 2])
        vare = sb("vare", [P, 2, NBLK])
        std = sb("std", [P, 2, NBLK])
        rstd = sb("rstd", [P, 2, NBLK])
        nmr = sb("nmr", [P, NBLK])
        gate_sb = sb("gate_sb", [P, 2, E])
        xnT = sb("xnT", [P, 2, QT])
        lg = sb("lg", [P, QT])
        lgT = lg[0:E, :]
        skip = lg
        ended, begun = (lg[:, k * SLOTS * E:(k + 1) * SLOTS * E].rearrange("p (s e) -> p s e", e=E) for k in range(2))
        logits = sb("logits", [P, NBLK, E])
        top = sb("top", [P, NBLK, 8])
        topi = sb("topi", [P, NBLK, 8], U32)
        topf = sb("topf", [P, NBLK, TOPK])
        iota_e = sb("iota_e", [P, QBLK, E])
        region = sb("region", [P, QBLK, E])
        hot = sb("hot", [P, NQ, TOPK, QBLK, E])
        mask = sb("mask", [P, NQ, QBLK, E])
        rank = sb("rank", [P, NQ, QBLK, E])
        carry = sb("carry", [P, E, QBLK])
        blocksum = sb("blocksum", [P, NQ, E, QBLK])
        upto = sb("upto", [P, NQ, E, QBLK])
        count = sb("count", [P, NQ, E])
        iota_k = sb("iota_k", [P, E, NBLK])
        over = sb("over", [P, E, NBLK])
        tiles = sb("tiles", [P, E])
        tile_end = sb("tile_end", [P, E])
        first_slot = sb("first_slot", [P, E])
        first_row = sb("first_row", [P, E])
        iota_8e = sb("iota_8e", [P, E])
        row_shift = sb("row_shift", [P, E])
        iota_s = sb("iota_s", [P, SLOTS, E])
        slot_f = sb("slot_f", [P, 2, SLOTS])
        slot_tab = sb("slot_tab", [P, 2, SLOTS], I32)
        place = sb("place", [P, NQ, QBLK, E])
        place_hot = sb("place_hot", [P, NQ, TOPK, QBLK, E])
        pos_f = sb("pos_f", [P, NQ, TOPK, QBLK])
        pos = sb("pos", [P, NQ, TOPK, QBLK], U32)
        ypos = sb("ypos", [P, NQ, TOPK, QBLK], U32)
        gap = sb("gap", [P, NBLK])
        egap = sb("egap", [P, NBLK])
        eden = sb("eden", [P, NBLK])
        wts = sb("wts", [P, TOPK, NBLK])

        spread_f = hC[:, :, :].rearrange("p i t -> p (i t)")
        sp_exp = [dA[:, h, :] for h in range(2)]
        xn = u[:, :, :, :].rearrange("p q h t -> p (q h t)").rearrange("p (t d) -> p t d", t=NBLK)
        silu_g, hid, hidT, xio = dA, dBu, hst, hC
        x_tile = [xio[:, i, 0:DX] for i in range(2)]
        xT_tile = [xio[:, i, DX:2 * DX].rearrange("p (k t) -> p k t", k=2) for i in range(2)]
        y_tile = [B_rep[:, 0, i * DX:(i + 1) * DX] for i in range(2)]
        dt_lo = xnT[0:DR, :, :]
        got = [zs, xn]

        PD = [stack.enter_context(nc.psum_tensor(f"PD{i}", [P, 512], F32)) for i in range(2)]
        PU = [stack.enter_context(nc.psum_tensor(f"PU{i}", [P, 512], F32)) for i in range(2)]
        PY = stack.enter_context(nc.psum_tensor("PY", [P, 2, QT], F32))
        PZ = [stack.enter_context(nc.psum_tensor(f"PZ{i}", [P, 512], F32)) for i in range(2)]
        bank = [PD[0][:, :], PD[1][:, :], PU[0][:, :], PU[1][:, :], PY[:, 0, :], PY[:, 1, :], PZ[0][:, :], PZ[1][:, :]]

        delta, du = ([t[:, h, :] for h in range(2)] for t in (dBu, hst))
        xprojT_ps = [bank[3][:, h * 64:h * 64 + DR + 2 * DS] for h in range(2)]
        dtwT_ps = [bank[3][0:DR, (h + 1) * P:(h + 2) * P] for h in range(2)]
        A_ps = bank[3][:, 3 * P:3 * P + NG * TPG]
        cols_ps = bank[3][:, 3 * P + NG * TPG:3 * P + NG * TPG + 6]
        CONV = [bank[i] for i in (0, 1, 2, 4)]
        DT = [bank[i][0:DR, :] for i in (5, 1)]
        BC = [[bank[6], bank[0]], [bank[5], bank[6]]]
        DRAW = [bank[i] for i in (3, 7, 2, 4)]

        x_slots = nc.dram_tensor("x_slots", [E * TOK, DX], F32, kind="Internal").ap()
        y_slots = nc.dram_tensor("y_slots", [SLOTS * P, DX], F32, kind="Internal").ap()

        ld = {n: sem("ld_" + n) for n in ("ctx", "inw", "convw", "small", "x", "gates", "w")}
        consts = sem("consts")
        tapw_ok, ctxT_ps, ctxT_ok, tapT_ps, tapT_ok = map(sem, ("tapw_ok", "ctxT_ps", "ctxT_ok", "tapT_ps", "tapT_ok"))
        smallT_ps, small_ok, Aexp_ok, Aneg_ok, spread_ok = map(sem, ("smallT_ps", "small_ok", "Aexp_ok", "Aneg_ok", "spread_ok"))
        tanh_ok, stats_ok, std_ok, rstd_ok, zs_ok = map(sem, ("tanh_ok", "stats_ok", "std_ok", "rstd_ok", "zs_ok"))
        conv_ps, u_ok, dt_ps, dt_ok, bc_ps, bc_ok, draw_ps, sp_raw, sp_exp_ok, sp_ln_ok, sp_dve, delta_ok, du_ok = map(
            sem, ("conv_ps", "u_ok", "dt_ps", "dt_ok", "bc_ps", "bc_ok", "draw_ps", "sp_raw", "sp_exp_ok", "sp_ln_ok",
                  "sp_dve", "delta_ok", "du_ok"))
        skip_ok, gz_ok, turned_ps = sem("skip_ok"), sem("gz_ok"), sem("turned_ps")
        dhi_ok, duhi_ok, dlo_ok, dulo_ok = map(sem, ("dhi_ok", "duhi_ok", "dlo_ok", "dulo_ok"))
        d_spread, du_spread, exp_done, dbu_done, scan_done, hc_done, y_done = map(
            sem, ("d_spread", "du_spread", "exp_done", "dbu_done", "scan_done", "hc_done", "y_done"))
        zero_ok, zeroed = sem("zero_ok"), sem("zeroed")
        x2_ok, stats2_ok, std2_ok, rstd2_ok, xn_ok, xnT_ps, xnT_ok, lgT_ps, lgT_ok, logit_ps, logit_ok = map(
            sem, ("x2_ok", "stats2_ok", "std2_ok", "rstd2_ok", "xn_ok", "xnT_ps", "xnT_ok", "lgT_ps", "lgT_ok", "logit_ps", "logit_ok"))
        route, mask_ok, rank_ps, rank_out, egap_ok, slots_ok, pos_ok, scattered = map(
            sem, ("route", "mask_ok", "rank_ps", "rank_out", "egap_ok", "slots_ok", "pos_ok", "scattered"))
        table_ok = sem("table_ok")
        gap_ok, cols_ok, ypos_ok = sem("gap_ok"), sem("cols_ok"), sem("ypos_ok")
        x_in = [sem("x_in0"), sem("x_in1")]
        xT_ps, xT_ok, g_ps, u_ps, silu_ok, hid_ok, hidT_ps, hidT_ok, y_ps, y_sb = map(
            sem, ("xT_ps", "xT_ok", "g_ps", "u_ps", "silu_ok", "hid_ok", "hidT_ps", "hidT_ok", "y_ps", "y_sb"))
        y_out = [sem("y_out0"), sem("y_out1")]
        gathered = [sem(f"gathered{i}") for i in range(NBLK)]
        comb = [sem("comb0"), sem("comb1")]
        stored = sem("stored")

        block = stack.enter_context(nc.Block())

        @block.sync
        def _(sp):
            sp.dma_start(ctx_sb, ctx_1024.rearrange("b (r p) d -> p (b r) d", p=P)).then_inc(ld["ctx"], 16)
            sp.dma_start(inw, in_proj_w.rearrange("(h p) d -> p h d", p=P)).then_inc(ld["inw"], 16)
            sp.dma_start(convw[:, :, :], conv_w.rearrange("(h p) k -> p h k", p=P)).then_inc(ld["convw"], 16)
            sp.dma_start(xs[:, :, :], x.rearrange("b (r p) d -> p (b r) d", p=P)).then_inc(ld["x"], 16)
            sp.wait_ge(ld["small"], 16 * 7)
            sp.wait_ge(ld["x"], 16)
            for e in range(E):
                sp.dma_start(W0[:, e, :, :], w0[e].rearrange("(k p) m -> p k m", p=P)).then_inc(ld["w"], 16)
                sp.dma_start(W1[:, e, :, :], w1[e].rearrange("(k p) m -> p k m", p=P)).then_inc(ld["w"], 16)
            sp.wait_ge(zero_ok, 1)
            for e in range(E):
                sp.dma_start(x_slots[e * TOK:(e + 1) * TOK, :].rearrange("(t p) d -> p t d", p=P),
                             zero[:, :].rearrange("p (o d) -> p o d", o=1).to_broadcast((P, NBLK, DX))).then_inc(zeroed, 16)
            sp.wait_ge(delta_ok, 2 * NQ)
            sp.wait_ge(conv_ps, 4)
            for e in range(E):
                sp.dma_start(WO[:, e, :, :], wo[e].rearrange("(k p) n -> p k n", p=P)).then_inc(ld["w"], 16)
            sp.wait_ge(scattered, 16 * TOPK * NBLK)

            def slot_in(s, i):
                tile = sp.value_load(slot_tab[0:1, 1, bass.ds(s, 1)], min_val=0, max_val=E * NBLK - 1)
                sp.dma_start(x_tile[i], x_slots[bass.ds(tile * P, P), :]).then_inc(x_in[i], 16)

            sp.wait_ge(slots_ok, 1)
            slot_in(0, 0)
            slot_in(1, 1)
            with sp.Fori(0, (SLOTS - 3) // 2) as t:
                for i in range(2):
                    sp.wait_ge(xT_ps, 2 * t + i + 1)
                    slot_in(2 * t + i + 2, i)
            sp.wait_ge(xT_ps, SLOTS - 2)
            slot_in(SLOTS - 1, (SLOTS - 1) % 2)
            for i in range(NBLK):
                sp.wait_ge(comb[1], i + 1)
                sp.dma_start(out[i // 2, (i % 2) * P:(i % 2 + 1) * P, :], xs[:, i, :]).then_inc(stored, 16)
            sp.wait_ge(stored, 16 * NBLK)

        @block.gpsimd
        def _(pool):
            pool.memset(ident[:, :], 0.0).then_inc(consts, 1)
            pool.memset(spread_f, 0.0).then_inc(consts, 1)
            pool.wait_ge(consts, 2)
            pool.affine_select(out=ident[:, :], in_=ident[:, :], compare_op=ALU.not_equal, fill=1.0, base=0,
                               pattern=[[-1, P]], channel_multiplier=1).then_inc(consts, 1)
            sv = spread_f.rearrange("p (j c n) -> p j c n", j=TPG, c=CH)
            for part in range(2):
                pool.affine_select(out=sv, in_=sv, compare_op=ALU.not_equal, fill=1.0, base=-GRP * part,
                                   pattern=[[-CH, TPG], [-1, CH], [0, DS]], channel_multiplier=1).then_inc(consts, 1)
                pool.wait_ge(consts, 4 + part)
            pool.memset(sum16[:, :, :], 1.0).then_inc(consts, 1)
            pool.memset(ones[:, :], 1.0).then_inc(consts, 1)
            pool.memset(before[:, :], 1.0).then_inc(consts, 1)
            pool.memset(carry[:, :, :], 1.0).then_inc(consts, 1)
            pool.wait_ge(consts, 9)
            pool.affine_select(out=sum16[:, :, :], in_=sum16[:, :, :], compare_op=ALU.is_ge, fill=0.0, base=0,
                               pattern=[[DS * CH, TPH], [-DS, P]], channel_multiplier=1).then_inc(consts, 1)
            pool.affine_select(out=before[:, :], in_=before[:, :], compare_op=ALU.is_gt, fill=0.0, base=0,
                               pattern=[[1, P]], channel_multiplier=-1).then_inc(consts, 1)
            pool.memset(carry[:, :, 0:1], 0.0).then_inc(consts, 1)
            for tab, pattern in ((iota_e, [[0, QBLK], [1, E]]), (region, [[0, QBLK], [TOK, E]]), (iota_k, [[0, E], [P, NBLK]]),
                                 (iota_s, [[1, SLOTS], [0, E]])):
                pool.iota(tab[:, :, :], pattern=pattern, base=0, channel_multiplier=0,
                          allow_small_or_imprecise_dtypes=True).then_inc(consts, 1)
            pool.iota(iota_8e[:, :], pattern=[[NBLK, E]], base=0, channel_multiplier=0,
                      allow_small_or_imprecise_dtypes=True).then_inc(consts, 1)
            pool.wait_ge(consts, 17)
            pool.affine_select(out=sum16[:, :, :], in_=sum16[:, :, :], compare_op=ALU.is_ge, fill=0.0, base=DS - 1,
                               pattern=[[-DS * CH, TPH], [DS, P]], channel_multiplier=-1).then_inc(consts, 1)

            pool.wait_ge(smallT_ps, 1)
            pool.memset(zero[:, :], 0.0).then_inc(zero_ok, 1)

            pool.sem_inc(hc_done, AHEAD)
            for q in range(NQ):
                pool.wait_ge(bc_ok, 2 * q + 2)
                with pool.Fori(q * TPH, (q + 1) * TPH) as t:
                    for i in range(2):
                        n = 2 * t + i
                        pool.wait_ge(scan_done, n + 1 + AHEAD)
                        pool.wait_ge(y_done, n + 1)
                        pool.tensor_tensor(hC[:, i, :], hst[:, i, :], C_rep[:, q, :],
                                           ALU.mult).then_inc(hc_done, 1)

            pool.wait_ge(zeroed, 16 * E)
            for q in range(NQ):
                pool.wait_ge(xn_ok, (q + 1) * QBLK)
                pool.wait_ge(pos_ok, q + 1)
                for k in range(TOPK):
                    for r in range(QBLK):
                        pool.indirect_dma_start(out=x_slots, out_offset=bass.IndirectOffsetOnAxis(ap=pos[:, q, k, r:r + 1], axis=0),
                                                in_=xn[:, q * QBLK + r, :], in_offset=None).then_inc(scattered, 16)
            pool.wait_ge(scattered, 16 * TOPK * NBLK)
            for i in range(2):
                pool.wait_ge(y_out[i], 16 * ((SLOTS + 1 - i) // 2))
            pool.wait_ge(ypos_ok, NQ)
            for i in range(NBLK):
                for k in range(TOPK):
                    pool.indirect_dma_start(out=got[k][:, i, :], out_offset=None, in_=y_slots,
                                            in_offset=bass.IndirectOffsetOnAxis(ap=ypos[:, i // QBLK, k, i % QBLK:i % QBLK + 1],
                                                                                axis=0)).then_inc(gathered[i], 16)

        @block.scalar
        def _(act):
            for v, vec in enumerate((conv_b, dt_proj_b, D)):
                act.dma_start(vec_rows[2 * v:2 * v + 2, :], vec.rearrange("(h p) -> h p", p=P)).then_inc(ld["small"], 16)
            act.dma_start(xproj_sb[:, :], x_proj_w).then_inc(ld["small"], 16)
            act.dma_start(dtw_sb[:, :, :], dt_proj_w.rearrange("(h p) r -> p h r", p=P)).then_inc(ld["small"], 16)
            act.dma_start(Alog_sb[:, :], A_log.rearrange("(j c) n -> j (c n)", c=CH)).then_inc(ld["small"], 16)
            act.dma_start(gate_sb[:, :, :], gate_w.rearrange("(k p) e -> p k e", p=P)).then_inc(ld["small"], 16)
            for i, gv in enumerate((g_xattn, g_ffn)):
                act.dma_start(gates[:, i:i + 1], gv.rearrange("(a n) -> a n", a=1).to_broadcast((P, 1))).then_inc(ld["gates"], 16)
            act.wait_ge(ld["gates"], 32)
            act.activation(tg[:, :], gates[:, :], ACT.Tanh).then_inc(tanh_ok, 1)
            for h in range(2):
                act.wait_ge(tapT_ps, h + 1)
                act.activation(tapwT[:, h, :, :].rearrange("p k e -> p (k e)"), bank[6 + h], ACT.Copy).then_inc(tapT_ok, 1)
            act.wait_ge(stats_ok, NBLK * 2 + 1)
            act.activation(std[:, 0, :], vare[:, 0, :], ACT.Sqrt).then_inc(std_ok, 1)
            act.wait_ge(cols_ok, 1)

            def silu_u(c):
                act.wait_ge(conv_ps, c + 1)
                act.activation(u[:, c // 2, c % 2, :], CONV[c], ACT.Silu, bias=cols[:, 0, c % 2:c % 2 + 1]).then_inc(u_ok, 1)

            def silu_z(i):
                act.activation(zs[:, i, :], xs[:, i, :], ACT.Silu, bias=nmr[:, i:i + 1],
                               scale=rstd[:, 0, i:i + 1]).then_inc(zs_ok, 1)

            silu_u(0)
            act.wait_ge(rstd_ok, 2)
            for c in range(1, 2 * NQ):
                for i in range(2):
                    silu_z(2 * (c - 1) + i)
                silu_u(c)
            for i in range(NBLK - 2, NBLK):
                silu_z(i)
            act.wait_ge(smallT_ps, 1)
            act.activation(Aexp[:, :], A_ps, ACT.Exp).then_inc(Aexp_ok, 1)
            for q in range(NQ):
                if q:
                    act.wait_ge(delta_ok, 2)
                for h in range(2):
                    act.wait_ge(draw_ps, 2 * q + h + 1)
                    act.activation(sp_relu[h], DRAW[2 * q + h], ACT.Relu, bias=cols[:, 1, h:h + 1]).then_inc(sp_raw, 1)
                    act.activation(sp_exp[h], DRAW[2 * q + h], ACT.Abs, bias=cols[:, 1, h:h + 1]).then_inc(sp_raw, 1)
                for h in range(2):
                    act.wait_ge(sp_raw, 4 * q + 2 * h + 2)
                    act.activation(sp_exp[h], sp_exp[h], ACT.Exp, scale=-1.0).then_inc(sp_exp_ok, 1)
                for h in range(2):
                    act.wait_ge(sp_exp_ok, 2 * q + h + 1)
                    act.activation(sp_ln[h], sp_exp[h], ACT.Ln, bias=1.0).then_inc(sp_ln_ok, 1)
                for h in range(2):
                    c = 2 * q + h
                    for parts, src, ready, done in ((d_parts, delta[h], delta_ok, dhi_ok), (du_parts, du[h], du_ok, duhi_ok)):
                        act.wait_ge(ready, c + 1)
                        for k in range(2):
                            rows = slice(GRP * k, GRP * (k + 1))
                            act.activation(parts[rows, q * NG + 2 * h + k, :], src[rows, :], ACT.Copy).then_inc(done, 1)
            act.wait_ge(Aneg_ok, 2)
            act.sem_inc(exp_done, AHEAD)

            def decay(at, end):
                with act.Fori(at // 2, end // 2) as t:
                    for i in range(2):
                        n = 2 * t + i
                        act.wait_ge(d_spread, n + 1)
                        act.wait_ge(scan_done, n + 1)
                        act.activation(dA[:, i, :].rearrange("p (b l) -> p b l", b=QB)[:, :, 1:L],
                                       PD[i][:, :].rearrange("p (b l) -> p b l", b=QB)[:, :, 1:L],
                                       ACT.Exp, scale=Aneg[:, bass.ds(n, 1)]).then_inc(exp_done, 1)

            def root(q):
                act.wait_ge(stats2_ok, (q + 1) * (2 * QBLK + 1))
                act.activation(std[:, 1, q * QBLK:(q + 1) * QBLK], vare[:, 1, q * QBLK:(q + 1) * QBLK], ACT.Sqrt).then_inc(std2_ok, 1)

            def exp_table():
                act.activation(Aexp[0:1, 0:1], tg[0:1, 0:1], ACT.Exp).then_inc(table_ok, 1)

            exp_table()
            decay(0, ROOT_AT)
            root(0)
            act.wait_ge(table_ok, 1)
            exp_table()
            decay(ROOT_AT, NQ * 2 * TPH)
            root(1)
            act.wait_ge(gap_ok, 1)
            act.activation(egap[:, :], gap[:, :], ACT.Exp).then_inc(egap_ok, 1)

            act.wait_ge(scattered, 16 * TOPK * NBLK)

            def xT_out(s, i):
                act.wait_ge(xT_ps, s + 1)
                if not (isinstance(s, int) and s < 2):
                    act.wait_ge(u_ps, s - 1)
                act.activation(xT_tile[i].rearrange("p k t -> p (k t)"), bank[6][:, i * DX:(i + 1) * DX], ACT.Copy).then_inc(xT_ok, 1)

            def silu(s, i):
                act.wait_ge(g_ps, s + 1)
                if not (isinstance(s, int) and s < 2):
                    act.wait_ge(hid_ok, s - 1)
                act.activation(silu_g[:, i, :], bank[i][:, :], ACT.Silu).then_inc(silu_ok, 1)

            def y_store(s, i, reused):
                act.wait_ge(y_ps, s + 1)
                if reused is not None:
                    act.wait_ge(y_out[i], reused)
                act.activation(y_tile[i], bank[7][:, i * DX:(i + 1) * DX], ACT.Copy).then_inc(y_sb, 1)
                act.wait_ge(y_sb, s + 1)
                act.dma_start(y_slots[bass.ds(s * P, P), :], y_tile[i]).then_inc(y_out[i], 16)

            xT_out(0, 0)
            xT_out(1, 1)
            silu(0, 0)
            for s in range(2):
                xT_out(s + 2, s)
                silu(s + 1, (s + 1) % 2)
                y_store(s, s, None)
            with act.Fori(1, (SLOTS - 3) // 2) as t:
                for i in range(2):
                    xT_out(2 * t + i + 2, i)
                    silu(2 * t + i + 1, (i + 1) % 2)
                    y_store(2 * t + i, i, 16 * t)
            for s in range(SLOTS - 3, SLOTS):
                if s + 2 < SLOTS:
                    xT_out(s + 2, s % 2)
                if s + 1 < SLOTS:
                    silu(s + 1, (s + 1) % 2)
                y_store(s, s % 2, 16 * (s // 2))

        @block.tensor
        def _(pe):
            pe.wait_ge(consts, 3)
            pe.wait_ge(ld["ctx"], 16)
            for t in range(NBLK):
                pe.transpose(bank[4 + t // 4][:, (t % 4) * P:(t % 4 + 1) * P], ctx_sb[:, t, :], ident[:, :]).then_inc(ctxT_ps, 1)
            for h in range(2):
                pe.wait_ge(tapw_ok, DC * (h + 1))
                for k in range(DC):
                    mm = pe.transpose(bank[6 + h][:, k * P:(k + 1) * P], tapw[:, h, k, :], ident[:, :])
                mm.then_inc(tapT_ps, 1)
            pe.wait_ge(ld["small"], 16 * 7)
            for h in range(2):
                pe.transpose(xprojT_ps[h], xproj_sb[:, h * P:(h + 1) * P], ident[0:DR + 2 * DS, 0:DR + 2 * DS])
                pe.transpose(dtwT_ps[h], dtw_sb[:, h, :], ident[:, :])
            pe.transpose(cols_ps, vec_rows[:, :], ident[0:6, 0:6])
            pe.transpose(A_ps, Alog_sb[:, :], ident[0:NG * TPG, 0:NG * TPG]).then_inc(smallT_ps, 1)
            pe.wait_ge(ctxT_ok, 3)
            for c in range(2 * NQ):
                q, h = divmod(c, 2)
                pe.wait_ge(tapT_ok, h + 1)
                for k in range(DC):
                    mm = pe.matmul(CONV[c].rearrange("p (b l) -> p b l", b=QB), tapwT[:, h, k, :],
                                   ctxT[:, q * QB:(q + 1) * QB, k:k + L], start=(k == 0), stop=(k == DC - 1))
                mm.then_inc(conv_ps, 1)

            def of_u(w, dest, q, done):
                for h in range(2):
                    mm = pe.matmul(dest, w[h], u[:, q, h, :], start=(h == 0), stop=(h == 1))
                mm.then_inc(done, 1)

            w_dt = [xprojT_dt[:, h, :] for h in range(2)]
            w_B, w_C = ([w[:, h, :, :].rearrange("p c n -> p (c n)") for h in range(2)] for w in (xprojT_B, xprojT_C))
            pe.wait_ge(small_ok, 5)
            pe.wait_ge(Aexp_ok, 1)
            for q in range(NQ):
                pe.wait_ge(u_ok, 2 * q + 2)
                if q:
                    pe.wait_ge(u_ok, 4)
                of_u(w_dt, DT[q], q, dt_ps)
                if q:
                    pe.wait_ge(dt_ok, 1)
                of_u(w_B, BC[q][0], q, bc_ps)
                pe.wait_ge(dt_ok, q + 1)
                for h in range(2):
                    pe.matmul(DRAW[2 * q + h], dtwT[:, h, :], dt_lo[:, q, :], start=True, stop=True).then_inc(draw_ps, 1)
                if q:
                    pe.wait_ge(bc_ok, 1)
                of_u(w_C, BC[q][1], q, bc_ps)

            def spread_tile(g, j, n):
                pe.wait_ge(exp_done, n + 1)
                pe.matmul(PD[j % 2][:, :], spread[:, j, :], d_parts[:, bass.ds(g, 1), :].rearrange("p o t -> p (o t)"),
                          start=True, stop=True).then_inc(d_spread, 1)
                pe.wait_ge(dbu_done, n + 1)
                pe.matmul(PU[j % 2][:, :], spread[:, j, :], du_parts[:, bass.ds(g, 1), :].rearrange("p o t -> p (o t)"),
                          start=True, stop=True).then_inc(du_spread, 1)

            def sum_states(h, j, n):
                pe.wait_ge(hc_done, n + 1 + AHEAD)
                pe.matmul(PY[:, bass.ds(h, 1), :].rearrange("p o t -> p (o t)"), sum16[:, j, :], hC[:, j % 2, :],
                          start=(j == 0), stop=(j == TPH - 1)).then_inc(y_done, 1)

            def half(q, it, last=False, hooks={}):
                if q:
                    pe.wait_ge(gz_ok, it - 1)
                for j in range(TPH):
                    n = it * TPH + j
                    if j + LEAD < TPH or not last:
                        spread_tile(it * 2 + (j + LEAD) // TPG, (j + LEAD) % TPG, n + LEAD)
                    sum_states(it - 2 * q, j, n)
                    if j in hooks:
                        hooks[j]()

            def turn_gz(q):
                pe.wait_ge(gz_ok, 2 * q + 2)
                if q:
                    pe.wait_ge(rank_out, 1)
                for r in range(QB):
                    for l in range(2):
                        for h in range(2):
                            mm = pe.transpose(PZ[r][:, l * DX + h * P:l * DX + (h + 1) * P],
                                              zs[:, q * QBLK + 2 * r + h, l * P:(l + 1) * P], ident[:, :])
                    mm.then_inc(turned_ps, 1)

            def turn_xn(q):
                pe.wait_ge(xn_ok, (q + 1) * QBLK)
                for k in range(2):
                    for r in range(QBLK):
                        mm = pe.transpose(PZ[k][:, r * P:(r + 1) * P], xn[:, q * QBLK + r, k * P:(k + 1) * P], ident[:, :])
                    mm.then_inc(xnT_ps, 1)

            def router(q):
                pe.wait_ge(xnT_ok, 2 * q + 2)
                for k in range(2):
                    mm = pe.matmul(PZ[0][0:E, :], gate_sb[:, k, :], xnT[:, k, :], start=(k == 0), stop=(k == 1))
                mm.then_inc(lgT_ps, 1)

            def turn_logits(q):
                pe.wait_ge(lgT_ok, q + 1)
                for r in range(QBLK):
                    mm = pe.transpose(PZ[1][:, r * E:(r + 1) * E], lgT[:, r * P:(r + 1) * P], ident[0:E, 0:E])
                mm.then_inc(logit_ps, 1)

            def ranks(q):
                pe.wait_ge(mask_ok, q + 1)
                m = mask[:, q, :, :].rearrange("p t e -> p (t e)")
                pe.matmul(PZ[0][:, 0:QBLK * E], before[:, :], m, start=True, stop=True)
                pe.matmul(PZ[0][:, 64:64 + QBLK * E], ones[:, :], m, start=True, stop=True).then_inc(rank_ps, 1)

            pe.wait_ge(dlo_ok, 4 * NQ)
            pe.wait_ge(dulo_ok, 4 * NQ)
            pe.wait_ge(dhi_ok, 4 * NQ)
            pe.wait_ge(duhi_ok, 4 * NQ)
            pe.wait_ge(spread_ok, 1)
            pe.wait_ge(bc_ok, 2 * NQ)
            pe.wait_ge(consts, 18)
            pe.sem_inc(y_done, AHEAD)
            for j in range(LEAD):
                spread_tile(0, j, j)
            with pe.Fori(0, 2) as it:
                half(0, it)
            half(1, 2, hooks={PE_POST[0]: lambda: turn_gz(0), PE_POST[1]: lambda: turn_xn(0)})
            half(1, 3, last=True, hooks={PE_POST[2]: lambda: router(0), PE_POST[3]: lambda: turn_logits(0),
                                         PE_POST[4]: lambda: ranks(0)})
            turn_gz(1)
            turn_xn(1)
            router(1)
            turn_logits(1)
            ranks(1)

            pe.wait_ge(slots_ok, 1)
            pe.wait_ge(ld["w"], 16 * 3 * E)

            def x_turn(s, i, loaded):
                pe.wait_ge(x_in[i], loaded)
                if not (isinstance(s, int) and s < 1):
                    pe.wait_ge(xT_ok, s)
                for k in range(2):
                    mm = pe.transpose(bank[6][:, i * DX + k * P:i * DX + (k + 1) * P], x_tile[i][:, k * P:(k + 1) * P], ident[:, :])
                mm.then_inc(xT_ps, 1)

            def product(W, dest, i, expert, done):
                for k in range(2):
                    mm = pe.matmul(dest[i][:, :], xT_tile[i][:, k, :], W[:, bass.ds(expert, 1), k, :].rearrange("p o m -> p (o m)"),
                                   start=(k == 0), stop=(k == 1))
                mm.then_inc(done, 1)

            def gate(s, i, expert):
                pe.wait_ge(xT_ok, s + 1)
                if not (isinstance(s, int) and s < 2):
                    pe.wait_ge(silu_ok, s - 1)
                product(W0, bank[0:2], i, expert, g_ps)

            def up(s, i, expert):
                if not (isinstance(s, int) and s < 2):
                    pe.wait_ge(hid_ok, s - 1)
                product(W1, bank[2:4], i, expert, u_ps)

            def hid_turn(s, i):
                pe.wait_ge(hid_ok, s + 1)
                if not (isinstance(s, int) and s < 2):
                    pe.wait_ge(hidT_ok, s - 1)
                for k in range(4):
                    mm = pe.transpose(bank[4 + i][:, k * P:(k + 1) * P], hid[:, i, k * P:(k + 1) * P], ident[:, :])
                mm.then_inc(hidT_ps, 1)

            def down(s, i, expert):
                pe.wait_ge(hidT_ok, s + 1)
                if not (isinstance(s, int) and s < 1):
                    pe.wait_ge(y_sb, s)
                for k in range(4):
                    mm = pe.matmul(bank[7][:, i * DX:(i + 1) * DX], hidT[:, i, k * P:(k + 1) * P],
                                   WO[:, bass.ds(expert, 1), k, :].rearrange("p o n -> p (o n)"), start=(k == 0), stop=(k == 3))
                mm.then_inc(y_ps, 1)

            def expert_of(s):
                return pe.value_load(slot_tab[0:1, 0, bass.ds(s, 1)], min_val=0, max_val=E - 1)

            def step(s, i, loaded, turn=True, nxt=True):
                now = expert_of(s)
                if turn:
                    x_turn(s + 2, i, loaded)
                if nxt:
                    follows = expert_of(s + 1)
                    gate(s + 1, 1 - i, follows)
                hid_turn(s, i)
                if nxt:
                    up(s + 1, 1 - i, follows)
                down(s, i, now)

            x_turn(0, 0, 16)
            x_turn(1, 1, 16)
            first = expert_of(0)
            gate(0, 0, first)
            up(0, 0, first)
            step(0, 0, 32)
            step(1, 1, 32)
            with pe.Fori(1, (SLOTS - 3) // 2) as t:
                for i in range(2):
                    step(2 * t + i, i, 16 * t + 32)
            step(SLOTS - 3, 0, 16 * ((SLOTS + 1) // 2))
            step(SLOTS - 2, 1, 0, turn=False)
            step(SLOTS - 1, 0, 0, turn=False, nxt=False)

        @block.vector
        def _(dve):
            dve.memset(ctxT[:, :, 0:DC - 1], 0.0).then_inc(ctxT_ok, 1)
            dve.wait_ge(ld["inw"], 16)
            dve.wait_ge(ld["convw"], 16)
            for h in range(2):
                for k in range(DC):
                    dve.tensor_scalar(tapw[:, h, k, :], inw[:, h, :], convw[:, h, k:k + 1], None, ALU.mult).then_inc(tapw_ok, 1)
            for q in range(NQ):
                dve.wait_ge(ctxT_ps, 4 * (q + 1))
                dve.tensor_copy(ctxT[:, q * QB:(q + 1) * QB, DC - 1:], bank[4 + q].rearrange("p (b l) -> p b l", b=QB)).then_inc(ctxT_ok, 1)
            dve.wait_ge(smallT_ps, 1)
            dve.tensor_copy(cols[:, :, :].rearrange("p v h -> p (v h)"), cols_ps).then_inc(cols_ok, 1)
            for h in range(2):
                dve.tensor_copy(xprojT_dt[:, h, :], xprojT_ps[h][:, 0:DR])
                for n, w in enumerate((xprojT_B, xprojT_C)):
                    src = xprojT_ps[h][:, DR + n * DS:DR + (n + 1) * DS].rearrange("p (o n) -> p o n", o=1).to_broadcast((P, CH, DS))
                    dve.tensor_copy(w[:, h, :, :], src).then_inc(small_ok, 1)
            dve.tensor_copy(dtwT[:, :, :].rearrange("r h e -> r (h e)"), bank[3][0:DR, P:3 * P]).then_inc(small_ok, 1)
            dve.wait_ge(ld["x"], 16)
            for i in range(NBLK):
                dve.bn_stats(stats[:, 0, i, :], xs[:, i, :]).then_inc(stats_ok, 1)
            for i in range(NBLK):
                dve.wait_ge(stats_ok, NBLK + i)
                dve.bn_aggr(mv[:, 0, i, :], stats[:, 0, i, :]).then_inc(stats_ok, 1)
            dve.wait_ge(stats_ok, 2 * NBLK)
            dve.tensor_scalar(vare[:, 0, :], mv[:, 0, :, 1], EPS, None, ALU.add).then_inc(stats_ok, 1)
            dve.wait_ge(std_ok, 1)
            dve.reciprocal(rstd[:, 0, :], std[:, 0, :]).then_inc(rstd_ok, 1)
            dve.wait_ge(rstd_ok, 1)
            dve.scalar_tensor_tensor(out=nmr[:, :], in0=mv[:, 0, :, 0], scalar=-1.0, in1=rstd[:, 0, :],
                                     op0=ALU.mult, op1=ALU.mult).then_inc(rstd_ok, 1)
            dve.wait_ge(consts, 5)
            dve.tensor_copy(spread[:, :, :].rearrange("p j m -> p (j m)"), spread_f).then_inc(spread_ok, 1)
            dve.wait_ge(Aexp_ok, 1)
            for k in range(NQ):
                dve.tensor_scalar(Aneg[:, k * NG * TPG:(k + 1) * NG * TPG], Aexp[:, :], -1.0, None, ALU.mult).then_inc(Aneg_ok, 1)

            def dt_out(q):
                dve.wait_ge(dt_ps, q + 1)
                dve.tensor_copy(dt_lo[:, q, :], DT[q]).then_inc(dt_ok, 1)

            def bc_out(q, n):
                dve.wait_ge(bc_ps, 2 * q + n + 1)
                dve.tensor_copy((B_rep, C_rep)[n][:, q, :], BC[q][n]).then_inc(bc_ok, 1)

            def log_terms(q):
                for h in range(2):
                    dve.wait_ge(sp_exp_ok, 2 * q + h + 1)
                    dve.tensor_scalar(sp_rest[h], sp_exp[h], 1.0, None, ALU.add).then_inc(sp_dve, 1)
                for h in range(2):
                    dve.wait_ge(sp_dve, 6 * q + h + 1)
                    dve.scalar_tensor_tensor(out=sp_rest[h], in0=sp_rest[h], scalar=1.0, in1=sp_exp[h],
                                             op0=ALU.subtract, op1=ALU.subtract).then_inc(sp_dve, 1)
                for h in range(2):
                    dve.wait_ge(sp_dve, 6 * q + h + 3)
                    dve.wait_ge(sp_ln_ok, 2 * q + h + 1)
                    dve.tensor_tensor(sp_rest[h], sp_ln[h], sp_rest[h], ALU.subtract).then_inc(sp_dve, 1)
                    if q:
                        dve.wait_ge(dhi_ok, 4)
                        dve.wait_ge(duhi_ok, 4)
                        dve.wait_ge(dlo_ok, 4)
                        dve.wait_ge(dulo_ok, 4)
                    dve.wait_ge(sp_dve, 6 * q + h + 5)
                    dve.tensor_tensor(delta[h], sp_rest[h], sp_relu[h], ALU.add).then_inc(delta_ok, 1)
                    dve.wait_ge(delta_ok, 2 * q + h + 1)
                    dve.tensor_tensor(du[h], delta[h], u[:, q, h, :], ALU.mult).then_inc(du_ok, 1)
                for h in range(2):
                    c = 2 * q + h
                    dve.wait_ge(du_ok, c + 1)
                    for parts, src, ready, done in ((d_parts, delta[h], dhi_ok, dlo_ok), (du_parts, du[h], duhi_ok, dulo_ok)):
                        for k in range(2):
                            rows, other = slice(GRP * k, GRP * (k + 1)), slice(GRP * (1 - k), GRP * (2 - k))
                            dve.wait_ge(ready, 2 * c + k + 1)
                            dve.tensor_tensor(parts[other, q * NG + 2 * h + k, :], src[rows, :],
                                              parts[rows, q * NG + 2 * h + k, :], ALU.subtract).then_inc(done, 1)

            dt_out(0)
            bc_out(0, 0)
            bc_out(0, 1)
            dt_out(1)
            log_terms(0)
            bc_out(1, 0)
            bc_out(1, 1)
            log_terms(1)
            dve.wait_ge(sp_ln_ok, 4)
            dve.wait_ge(sp_dve, 12)
            dve.memset(dA[:, :, :].rearrange("p i (b l) -> p (i b) l", b=QB)[:, :, 0:1], 0.0).then_inc(scan_done, AHEAD)

            def drive(q, j, n):
                dve.wait_ge(du_spread, n + 1)
                dve.wait_ge(scan_done, n + 1)
                dve.tensor_tensor(dBu[:, j % 2, :], PU[j % 2][:, :], B_rep[:, q, :], ALU.mult).then_inc(dbu_done, 1)

            def scan(j, n):
                dve.wait_ge(exp_done, n + 1 + AHEAD)
                dve.wait_ge(dbu_done, n + 1 + AHEAD)
                dve.wait_ge(hc_done, n + 1)
                dve.tensor_tensor_scan(hst[:, j % 2, :], dA[:, j % 2, :], dBu[:, j % 2, :], 0.0,
                                       ALU.mult, ALU.add).then_inc(scan_done, 1)

            def pair(q, n, after):
                drive(q, 1, n + 1)
                scan(0, n)
                if after is not None:
                    drive(after, 0, n + 2)
                scan(1, n + 1)

            def tiles_to(q, at, end):
                whole = min(end, (q + 1) * 2 * TPH - 2)
                if whole > at:
                    with dve.Fori(at // 2, whole // 2) as t:
                        pair(q, 2 * t, q)
                if whole < end:
                    pair(q, whole, q + 1 if q + 1 < NQ else None)
                return end

            def run(q, at, *work):
                for after, do in work:
                    at = tiles_to(q, at, after)
                    do()
                tiles_to(q, at, (q + 1) * 2 * TPH)

            def gated(q, h, it):
                dve.wait_ge(y_done, AHEAD + (it + 1) * TPH)
                if it:
                    dve.wait_ge(gz_ok, it)
                yb = PY[:, bass.ds(h, 1), :].rearrange("p o t -> p (o t)")
                uh = u[:, q, bass.ds(h, 1), :].rearrange("p o t -> p (o t)")
                dve.scalar_tensor_tensor(out=skip[:, :], in0=uh, scalar=cols[:, 2, bass.ds(h, 1)], in1=yb,
                                         op0=ALU.mult, op1=ALU.add).then_inc(skip_ok, 1)
                dve.wait_ge(skip_ok, it + 1)
                zh = zs[:, :, :].rearrange("p (r h) l -> p h r l", h=2)[:, bass.ds(h, 1), 2 * q:2 * q + 2, :].rearrange("p o r l -> p (o r) l")
                dve.tensor_tensor(zh, skip[:, :].rearrange("p (r l) -> p r l", r=QB), zh, ALU.mult).then_inc(gz_ok, 1)

            def residual(q):
                for r in range(QB):
                    b = q * QB + r
                    dve.wait_ge(turned_ps, b + 1)
                    xb = xs[:, 2 * b:2 * b + 2, :].rearrange("p t d -> p (t d)")
                    dve.scalar_tensor_tensor(out=xb, in0=PZ[r][:, :], scalar=tg[:, 0:1], in1=xb,
                                             op0=ALU.mult, op1=ALU.add).then_inc(x2_ok, 1)
                base = q * (2 * QBLK + 1)
                for r in range(QBLK):
                    dve.wait_ge(x2_ok, q * QB + r // 2 + 1)
                    dve.bn_stats(stats[:, 1, q * QBLK + r, :], xs[:, q * QBLK + r, :]).then_inc(stats2_ok, 1)
                for r in range(QBLK):
                    dve.wait_ge(stats2_ok, base + QBLK + r)
                    dve.bn_aggr(mv[:, 1, q * QBLK + r, :], stats[:, 1, q * QBLK + r, :]).then_inc(stats2_ok, 1)
                dve.wait_ge(stats2_ok, base + 2 * QBLK)
                cut = slice(q * QBLK, (q + 1) * QBLK)
                dve.tensor_scalar(vare[:, 1, cut], mv[:, 1, cut, 1], EPS, None, ALU.add).then_inc(stats2_ok, 1)

            def normed(q):
                cut = slice(q * QBLK, (q + 1) * QBLK)
                dve.wait_ge(std2_ok, q + 1)
                dve.reciprocal(rstd[:, 1, cut], std[:, 1, cut]).then_inc(rstd2_ok, 1)
                dve.wait_ge(rstd2_ok, q + 1)
                for r in range(QBLK):
                    i = q * QBLK + r
                    dve.tensor_scalar(xn[:, i, :], xs[:, i, :], mv[:, 1, i, 0:1], rstd[:, 1, i:i + 1],
                                      ALU.subtract, ALU.mult).then_inc(xn_ok, 1)

            def xnT_out(q):
                for k in range(2):
                    dve.wait_ge(xnT_ps, 2 * q + k + 1)
                    dve.tensor_copy(xnT[:, k, :], PZ[k][:, :]).then_inc(xnT_ok, 1)

            def lgT_out(q):
                dve.wait_ge(lgT_ps, q + 1)
                dve.wait_ge(gz_ok, 3 + q)
                dve.tensor_copy(lgT[:, :], PZ[0][0:E, :]).then_inc(lgT_ok, 1)

            steps = [0]

            def link(ins):
                ins.then_inc(route, 1)
                steps[0] += 1
                dve.wait_ge(route, steps[0])

            def best_two(q):
                cut = slice(q * QBLK, (q + 1) * QBLK)
                dve.wait_ge(logit_ps, q + 1)
                link(dve.tensor_copy(logits[:, cut, :].rearrange("p t e -> p (t e)"), PZ[1][:, 0:QBLK * E]))
                for r in range(QBLK):
                    ins = dve.max(top[:, q * QBLK + r, :], logits[:, q * QBLK + r, :])
                    if r < QBLK - 1:
                        ins.then_inc(route, 1)
                        steps[0] += 1
                link(ins)
                for r in range(QBLK):
                    ins = dve.max_index(topi[:, q * QBLK + r, :], top[:, q * QBLK + r, :], logits[:, q * QBLK + r, :])
                    if r < QBLK - 1:
                        ins.then_inc(route, 1)
                        steps[0] += 1
                link(ins)
                link(dve.tensor_copy(topf[:, cut, :], topi[:, cut, 0:TOPK]))
                for k in range(TOPK):
                    ins = dve.tensor_tensor(hot[:, q, k, :, :], iota_e[:, :, :], topf[:, cut, k:k + 1].to_broadcast((P, QBLK, E)), ALU.is_equal)
                    if k == 0:
                        ins.then_inc(route, 1)
                        steps[0] += 1
                link(ins)
                dve.tensor_tensor(mask[:, q, :, :], hot[:, q, 0, :, :], hot[:, q, 1, :, :], ALU.add).then_inc(mask_ok, 1)

            def rows_of(q, start, dest, done):
                pv = place[:, q, :, :]
                link(dve.tensor_tensor(pv, rank[:, q, :, :], start, ALU.add))
                for k in range(TOPK):
                    ins = dve.tensor_tensor(place_hot[:, q, k, :, :], hot[:, q, k, :, :], pv, ALU.mult)
                    if k == 0:
                        ins.then_inc(route, 1)
                        steps[0] += 1
                link(ins)
                link(dve.tensor_reduce(pos_f[:, q, :, :].rearrange("p k t -> p (k t)"),
                                       place_hot[:, q, :, :, :].rearrange("p k t e -> p (k t) e"), AX_X, ALU.add))
                dve.tensor_copy(dest[:, q, :, :], pos_f[:, q, :, :]).then_inc(done, 1)

            def places(q):
                dve.wait_ge(rank_ps, q + 1)
                dve.wait_ge(consts, 18)
                sums = blocksum[:, q, :, :]
                dve.tensor_copy(rank[:, q, :, :].rearrange("p t e -> p (t e)"), PZ[0][:, 0:QBLK * E]).then_inc(rank_out, 1)
                dve.wait_ge(rank_out, 2 * q + 1)
                dve.tensor_copy(sums, PZ[0][:, 64:64 + QBLK * E].rearrange("p (t e) -> p e t", e=E)).then_inc(rank_out, 1)
                dve.wait_ge(rank_out, 2 * q + 2)
                link(dve.tensor_tensor_scan(upto[:, q, :, :].rearrange("p e t -> p (e t)"), carry[:, :, :].rearrange("p e t -> p (e t)"),
                                            sums.rearrange("p e t -> p (e t)"), 0.0, ALU.mult, ALU.add))
                if q == 0:
                    link(dve.tensor_copy(count[:, 0, :], upto[:, 0, :, QBLK - 1]))
                else:
                    link(dve.tensor_tensor(count[:, 1, :], upto[:, 1, :, QBLK - 1], count[:, 0, :], ALU.add))
                link(dve.tensor_tensor(upto[:, q, :, :], upto[:, q, :, :], sums, ALU.subtract))
                link(dve.tensor_tensor(rank[:, q, :, :], rank[:, q, :, :], upto[:, q, :, :].rearrange("p e t -> p t e"), ALU.add))
                if q:
                    link(dve.tensor_tensor(rank[:, q, :, :], rank[:, q, :, :],
                                           count[:, 0, :].rearrange("p (o e) -> p o e", o=1).to_broadcast((P, QBLK, E)), ALU.add))
                rows_of(q, region[:, :, :], pos, pos_ok)

            dve.sem_inc(dbu_done, AHEAD)
            drive(0, 0, 0)
            run(0, 0, (GATE_AT[0], lambda: gated(0, 0, 0)))
            run(1, 2 * TPH, (GATE_AT[1], lambda: gated(0, 1, 1)), (RESIDUAL_AT, lambda: residual(0)), (NORM_AT, lambda: normed(0)),
                (XNT_AT, lambda: xnT_out(0)), (GATE_AT[2], lambda: gated(1, 0, 2)), (LGT_AT, lambda: lgT_out(0)),
                (BEST_AT, lambda: best_two(0)), (PLACE_AT, lambda: places(0)))
            gated(1, 1, 3)
            residual(1)
            normed(1)
            xnT_out(1)
            lgT_out(1)
            best_two(1)
            places(1)

            dve.tensor_tensor(gap[:, :], top[:, :, 1], top[:, :, 0], ALU.subtract).then_inc(gap_ok, 1)
            cnt = count[:, 1, :].rearrange("p (e o) -> p e o", o=1).to_broadcast((P, E, NBLK))
            link(dve.tensor_tensor(over[:, :, :], cnt, iota_k[:, :, :], ALU.is_gt))
            link(dve.tensor_reduce(tiles[:, :], over[:, :, :], AX_X, ALU.add))
            link(dve.tensor_tensor_scan(tile_end[:, :], ones[:, 0:E], tiles[:, :], 0.0, ALU.mult, ALU.add))
            link(dve.tensor_tensor(first_slot[:, :], tile_end[:, :], tiles[:, :], ALU.subtract))
            per_slot = lambda v: v[:, :].rearrange("p (o e) -> p o e", o=1).to_broadcast((P, SLOTS, E))
            link(dve.tensor_tensor(ended[:, :, :], iota_s[:, :, :], per_slot(tile_end), ALU.is_ge))
            link(dve.tensor_tensor(begun[:, :, :], iota_s[:, :, :], per_slot(first_slot), ALU.is_ge))
            link(dve.tensor_reduce(slot_f[:, 0, :], ended[:, :, :], AX_X, ALU.add))
            link(dve.tensor_tensor(row_shift[:, :], iota_8e[:, :], first_slot[:, :], ALU.subtract))
            link(dve.tensor_tensor(begun[:, :, :], begun[:, :, :], ended[:, :, :], ALU.subtract))
            link(dve.tensor_tensor(begun[:, :, :], begun[:, :, :], per_slot(row_shift), ALU.mult))
            link(dve.tensor_reduce(slot_f[:, 1, :], begun[:, :, :], AX_X, ALU.add))
            link(dve.tensor_tensor(slot_f[:, 1, :], slot_f[:, 1, :], iota_s[:, :, 0], ALU.add))
            link(dve.tensor_scalar(slot_f[:, 0, :], slot_f[:, 0, :], float(E - 1), None, ALU.min))
            dve.tensor_copy(slot_tab[:, :, :], slot_f[:, :, :]).then_inc(slots_ok, 1)
            link(dve.tensor_scalar(first_row[:, :], first_slot[:, :], float(P), None, ALU.mult))
            for q in range(NQ):
                dve.wait_ge(pos_ok, q + 1)
                rows_of(q, first_row[:, :].rearrange("p (o e) -> p o e", o=1).to_broadcast((P, QBLK, E)), ypos, ypos_ok)
            dve.wait_ge(egap_ok, 1)
            link(dve.tensor_scalar(eden[:, :], egap[:, :], 1.0, None, ALU.add))
            link(dve.reciprocal(eden[:, :], eden[:, :]))
            link(dve.tensor_scalar(wts[:, 0, :], eden[:, :], tg[:, 1:2], None, ALU.mult))
            link(dve.tensor_tensor(wts[:, 1, :], wts[:, 0, :], egap[:, :], ALU.mult))

            def hidden(s, i, used):
                dve.wait_ge(silu_ok, s + 1)
                dve.wait_ge(u_ps, s + 1)
                if used is not None:
                    dve.wait_ge(hidT_ps, used)
                dve.tensor_tensor(hid[:, i, :], bank[2 + i][:, :], silu_g[:, i, :], ALU.mult).then_inc(hid_ok, 1)

            def turned(s, i, used):
                dve.wait_ge(hidT_ps, s + 1)
                if used is not None:
                    dve.wait_ge(y_ps, used)
                dve.tensor_copy(hidT[:, i, :], bank[4 + i][:, :]).then_inc(hidT_ok, 1)

            for s in range(2):
                hidden(s, s, None)
                turned(s, s, None)
            with dve.Fori(1, (SLOTS - 1) // 2) as t:
                for i in range(2):
                    hidden(2 * t + i, i, 2 * t + i - 1)
                    turned(2 * t + i, i, 2 * t + i - 1)
            hidden(SLOTS - 1, 0, SLOTS - 2)
            turned(SLOTS - 1, 0, SLOTS - 2)

            for i in range(NBLK):
                dve.wait_ge(gathered[i], 16 * TOPK)
                for k in range(TOPK):
                    dve.scalar_tensor_tensor(out=xs[:, i, :], in0=got[k][:, i, :], scalar=wts[:, k, i:i + 1],
                                             in1=xs[:, i, :], op0=ALU.mult, op1=ALU.add).then_inc(comb[k], 1)
                    if k == 0:
                        dve.wait_ge(comb[0], i + 1)


INPUTS = ("x", "ctx_1024", "g_xattn", "g_ffn", "L0_xattn_in_proj_w", "L0_xattn_conv_w", "L0_xattn_conv_b",
          "L0_xattn_x_proj_w", "L0_xattn_dt_proj_w", "L0_xattn_dt_proj_b", "L0_xattn_A_log", "L0_xattn_D",
          "L0_ffn_gate_w", "L0_ffn_w0", "L0_ffn_w1", "L0_ffn_wo")


def kernel(**inputs):
    import concourse.bacc as bacc
    from concourse.bass_utils import run_bass_kernel_spmd

    nc = bacc.Bacc("TRN2", target_bir_lowering=False, num_devices=1)
    arrays, args = {}, []
    for name in INPUTS:
        a = np.ascontiguousarray(inputs[name])
        arrays["in_" + name] = a
        args.append(nc.dram_tensor("in_" + name, a.shape, mybir.dt.from_np(a.dtype), kind="ExternalInput").ap())
    out = nc.dram_tensor("out", (B, L, DX), F32, kind="ExternalOutput").ap()
    build(nc, *args, out)
    result = run_bass_kernel_spmd(nc, [arrays], core_ids=[0])
    return result.results[0]["out"]
```

```python
from contextlib import ExitStack

import numpy as np

import concourse.bass as bass
from concourse import mybir

F32 = mybir.dt.float32
F32R = mybir.dt.float32r
I32 = mybir.dt.int32
U32 = mybir.dt.uint32
ALU = mybir.AluOpType
ACT = mybir.ActivationFunctionType
AX_X = mybir.AxisListType.X

P = 128
B, L, DX = 4, 256, 256
DM, DI, DS, DC, DR = 128, 256, 16, 4, 8
E, MH, TOPK = 8, 512, 2
TOK = B * L
NBLK = TOK // P
NQ = 2
QB = B // NQ
QT = QB * L
QBLK = QT // P
CH = P // DS
GRP = 64
NG = DI // GRP
TPG = GRP // CH
TPH = 2 * TPG
SLOTS = (TOK * TOPK - E) // P + E
EPS = 1e-5
PE_POST = (34, 44, 48, 51)
GATE_AT = (20, 36, 52)
RESIDUAL_AT = (38, 40)
VARIANCE_AT = 41
RSTD_AT = 43
BEST_AT = 53
PLACE_AT = 57
ROOT_AT = 42
NORM_AT = (44, 46)
XNT_AT = (48, 50)
LEAD = 4
ACT_UPPER = [(2, 1, 0), (2, 1, 1), (4, 1, 2), (4, 1, 3)] + [(4 * c + 4 + m // 2 * 2, c, m) for c in (2, 3) for m in range(4)]
POOL_LOWER = [(4, (1, 0)), (8, (1, 1)), (12, (2, 0)), (16, (2, 1)), (20, (3, 0))]
DVE_SPLIT = [(4, 1, 2), (6, 1, 3), (10, 2, None), (14, 3, None), (18, 2, 2), (18, 2, 3),
             (22, 3, 1), (22, 3, 2), (24, 3, 3)]
UNROLL = 6
DVE_EARLY, DVE_MIDDLE, DVE_W0 = 3, 5, 7
WARM = (5, 1, 4, 3)
POOL_BLOCKS = (1, 3, 5)
DVE_BLOCKS = tuple(i for i in range(NBLK) if i not in POOL_BLOCKS)
COLS = SLOTS + SLOTS % 2
AHEAD = 2
RING = 4


def build(nc, x, ctx_1024, g_xattn, g_ffn, in_proj_w, conv_w, conv_b, x_proj_w, dt_proj_w, dt_proj_b,
          A_log, D, gate_w, w0, w1, wo, out):
    stack = ExitStack()
    with stack:
        def sb(name, shape, dt=F32):
            return stack.enter_context(nc.sbuf_tensor(name, shape, dt))

        def sem(name):
            return stack.enter_context(nc.semaphore(name))

        at_W = -(-nc.sbuf_base // 32) * 32
        W0 = sb("W0", [P, E, 2, MH])
        W1 = sb("W1", [P, E, 2, MH])
        WO = sb("WO", [P, E, 4, DX])
        early = WO[:, :, :, :].rearrange("p e k n -> p (e k n)")
        taken = [0]

        def early_part(n):
            taken[0] += n
            return early[:, taken[0] - n:taken[0]]

        ctx_sb = early_part(NBLK * DM).rearrange("p (t d) -> p t d", t=NBLK)
        ctxT = early_part(B * (L + DC - 1)).rearrange("p (b l) -> p b l", b=B)
        tapw = early_part(2 * DC * DM).rearrange("p (h k d) -> p h k d", h=2, k=DC)
        tapwT = early_part(2 * DC * P).rearrange("p (h k e) -> p h k e", h=2, k=DC)
        sp_relu, sp_ln, sp_rest = ([early_part(QT) for h in range(2)] for _ in range(3))
        flat = lambda t: t.rearrange("p a b -> p (a b)")
        for terms, buf in ((sp_relu, flat(ctx_sb)), (sp_ln, tapw.rearrange("p h k d -> p (h k d)")), (sp_rest, flat(ctxT))):
            terms += [buf[:, h * QT:(h + 1) * QT] for h in range(2)]
        inw = early_part(2 * DM).rearrange("p (h d) -> p h d", h=2)
        inwT = early_part(2 * P)
        assert taken[0] <= E * 4 * DX

        at_W0_hi = nc.sbuf_base
        d_parts = sb("d_parts", [P, NQ * NG, QT], F32R)
        du_parts = sb("du_parts", [P, NQ * NG, QT], F32R)
        at_W1_hi = nc.sbuf_base
        zs = sb("zs", [P, NBLK, DX])
        B_rep = sb("B_rep", [P, NQ, QT])
        C_rep = sb("C_rep", [P, NQ, QT])
        sum16 = sb("sum16", [P, TPH, P])
        spread = sb("spread", [P, TPG, P], F32R)
        xnT = sb("xnT", [P, 2, QT])
        assert at_W1_hi - at_W0_hi == nc.sbuf_base - at_W1_hi == E * 2 * MH * 4
        dA = sb("dA", [P, 2, QT])
        at_states = nc.sbuf_base
        states = sb("states", [P, RING, QT])
        at_hC = nc.sbuf_base
        hC = sb("hC", [P, 2, QT])
        at_u = nc.sbuf_base
        u = sb("u", [P, NQ, 2, QT])
        xn = u[:, :, :, :].rearrange("p q h t -> p (q h t)").rearrange("p (t d) -> p t d", t=NBLK)
        xs = sb("xs", [P, NBLK, DX])
        ident = sb("ident", [P, P])
        ones = sb("ones", [P, P])
        before = sb("before", [P, P])
        Aneg = sb("Aneg", [P, NQ * NG * TPG])
        Aexp = sb("Aexp", [P, NG * TPG])
        Alog_sb = sb("Alog_sb", [NG * TPG, P])
        xprojT_B = sb("xprojT_B", [P, 2, CH, DS])
        xprojT_C = sb("xprojT_C", [P, 2, CH, DS])
        xprojT_dt = sb("xprojT_dt", [P, 2, DR])
        dtw_sb = sb("dtw_sb", [P, 2, DR])
        dtwT = sb("dtwT", [DR, 2, P])
        convw = sb("convw", [P, 2, DC])
        cols = sb("cols", [P, 3, 2])
        scratch = sb("scratch", [1, 1])
        vec_rows = sb("vec_rows", [6, P])
        gates = sb("gates", [P, 2])
        tg = sb("tg", [P, 2])
        stats = sb("stats", [P, 2, NBLK, 6])
        mv = sb("mv", [P, 2, NBLK, 2])
        vare = sb("vare", [P, 2, NBLK])
        std = sb("std", [P, 2, NBLK])
        rstd = sb("rstd", [P, 2, NBLK])
        nmr = sb("nmr", [P, NBLK])
        gate_sb = sb("gate_sb", [P, 2, E])
        lg = sb("lg", [P, QT])
        xproj_sb = lg[0:DR + 2 * DS, 0:DX]
        skip = lg
        ended = lg[:, 0:SLOTS * E].rearrange("p (s e) -> p s e", e=E)
        logits = sb("logits", [P, NBLK, E])
        top = sb("top", [P, NBLK, 8])
        topi = sb("topi", [P, NBLK, 8], U32)
        topf = sb("topf", [P, NBLK, TOPK])
        iota_e = sb("iota_e", [P, QBLK, E])
        result_id = sb("result_id", [P, NQ, TOPK, QBLK])
        iota_row = sb("iota_row", [P, P])
        spare_id = sb("spare_id", [P, 1])
        hot = sb("hot", [P, NQ, TOPK, QBLK, E])
        mask = sb("mask", [P, NQ, QBLK, E])
        rank = sb("rank", [P, NQ, QBLK, E])
        carry = sb("carry", [P, E, QBLK])
        blocksum = sb("blocksum", [P, NQ, E, QBLK])
        upto = sb("upto", [P, NQ, E, QBLK])
        count = sb("count", [P, NQ, E])
        iota_k = sb("iota_k", [P, E, NBLK])
        over = sb("over", [P, E, NBLK])
        tiles = sb("tiles", [P, E])
        tile_end = sb("tile_end", [P, E])
        first_slot = sb("first_slot", [P, E])
        iota_s = sb("iota_s", [P, SLOTS, E])
        iota_c = sb("iota_c", [P, 1, COLS])
        slot_f = sb("slot_f", [P, SLOTS])
        slot_tab = sb("slot_tab", [P, SLOTS], I32)
        picked = sb("picked", [P, NQ, TOPK, QBLK, E])
        first_of = sb("first_of", [P, NQ * TOPK * QBLK, E])
        rank_f = sb("rank_f", [P, NQ, TOPK, QBLK])
        rank_i = sb("rank_i", [P, NQ, TOPK, QBLK], I32)
        row_i = sb("row_i", [P, NQ, TOPK, QBLK], I32)
        row_f = sb("row_f", [P, NQ, TOPK, QBLK])
        tile_i = sb("tile_i", [P, NQ, TOPK, QBLK], I32)
        slot_of = sb("slot_of", [P, NQ * TOPK * QBLK])
        spare = sb("spare", [P, COLS])
        y_at = sb("y_at", [P, COLS], U32)
        x_at = sb("x_at", [P, COLS], U32)
        gap = sb("gap", [P, NBLK])
        egap = sb("egap", [P, NBLK])
        eden = sb("eden", [P, NBLK])
        wts = sb("wts", [P, TOPK, NBLK])

        spread_f = hC[:, :, :].rearrange("p i t -> p (i t)")
        sp_exp = [dA[:, h, :] for h in range(2)] + [tapwT[:, h, :, :].rearrange("p k e -> p (k e)") for h in range(2)]
        delta, du = sp_rest, sp_ln
        hid = dA
        def overlay(name, shape, offset):
            return nc.alloc_sbuf_tensor_at(name, shape, F32R, offset=offset)

        x_tile = [spread_f[:, i * DX:(i + 1) * DX] for i in range(2)]
        row_hot = overlay("row_hot", [P, NQ * TOPK * QBLK, P], at_states)
        slot_id = overlay("slot_id", [P, NQ * TOPK * QBLK, COLS], at_hC + 2 * DX * 4)
        xT_hi_t = overlay("xT_hi", [P, 2, 2, P], at_states + QT * 4)
        xT_lo_t = overlay("xT_lo", [P, 2, 2, P], at_states)
        hidT_hi, hidT_lo = (overlay(n, [P, 4, P], at_states + b * QT * 4) for n, b in (("hidT_hi", 2), ("hidT_lo", 3)))
        WO_hi, WO_lo = (overlay(n, [P, 4, DX], at_u + b * 4 * DX * 4) for n, b in (("WO_hi", 0), ("WO_lo", 1)))
        xT_hi, xT_lo = ([t[:, i, :, :] for i in range(2)] for t in (xT_hi_t, xT_lo_t))
        W0_hi, W1_hi = overlay("W0_hi", [P, E, 2, MH], at_W0_hi), overlay("W1_hi", [P, E, 2, MH], at_W1_hi)
        W0_lo, W1_lo = overlay("W0_lo", [P, E, 2, MH], at_W), overlay("W1_lo", [P, E, 2, MH], at_W + E * 2 * MH * 4)
        y_tile = [lg[:, i * DX:(i + 1) * DX] for i in range(2)]
        dt_lo = xnT[0:DR, :, :]
        got = [w[:, 0:2, :, :].rearrange("p e k m -> p (e k m)").rearrange("p (t d) -> p t d", t=NBLK) for w in (W0, W1)]

        PD = [stack.enter_context(nc.psum_tensor(f"PD{i}", [P, 512], F32)) for i in range(2)]
        PU = [stack.enter_context(nc.psum_tensor(f"PU{i}", [P, 512], F32)) for i in range(2)]
        PY = stack.enter_context(nc.psum_tensor("PY", [P, 2, QT], F32))
        PZ = [stack.enter_context(nc.psum_tensor(f"PZ{i}", [P, 512], F32)) for i in range(2)]
        bank = [PD[0][:, :], PD[1][:, :], PU[0][:, :], PU[1][:, :], PY[:, 0, :], PY[:, 1, :], PZ[0][:, :], PZ[1][:, :]]

        xprojT_ps = [bank[3][:, h * 64:h * 64 + DR + 2 * DS] for h in range(2)]
        dtwT_ps = [bank[3][0:DR, (h + 1) * P:(h + 2) * P] for h in range(2)]
        A_ps = bank[3][:, 3 * P:3 * P + NG * TPG]
        cols_ps = bank[3][:, 3 * P + NG * TPG:3 * P + NG * TPG + 6]
        inwT_ps = bank[0][:, 0:2 * P]
        CONV = [bank[i] for i in (0, 1)]
        XI = [bank[i] for i in (2, 4)]
        DT = [bank[i][0:DR, :] for i in (5, 1)]
        BC = [[bank[6], bank[0]], [bank[5], bank[6]]]
        DRAW = [bank[i] for i in (3, 7, 2, 4)]

        x_rows = nc.dram_tensor("x_rows", [TOK, DX], F32, kind="Internal").ap()
        y_rows = nc.dram_tensor("y_rows", [TOPK * TOK + P, DX], F32, kind="Internal").ap()

        ld = {n: sem("ld_" + n) for n in ("ctx", "inw", "convw", "small", "x", "gates", "w")}
        consts = sem("consts")
        tapw_ok, ctxT_ps, ctxT_ok, tapT_ps, tapT_ok = map(sem, ("tapw_ok", "ctxT_ps", "ctxT_ok", "tapT_ps", "tapT_ok"))
        smallT_ps, small_ok, Alog_ok, Aexp_ok, Aneg_ok, spread_ok = map(sem, ("smallT_ps", "small_ok", "Alog_ok", "Aexp_ok", "Aneg_ok", "spread_ok"))
        tanh_ok, stats_ok, std_ok, rstd_ok, zs_ok = map(sem, ("tanh_ok", "stats_ok", "std_ok", "rstd_ok", "zs_ok"))
        inwT_ps_ok, inwT_ok, xi_ps = map(sem, ("inwT_ps_ok", "inwT_ok", "xi_ps"))
        taps_ok = [sem("taps_ok0"), sem("taps_ok1")]
        conv_ps, u_ok, dt_ps, dt_ok, bc_ps, draw_ps, abs_ok, relu_ok, sp_exp_ok, sp_ln_ok, one_plus, rest_ok, base_ok = map(
            sem, ("conv_ps", "u_ok", "dt_ps", "dt_ok", "bc_ps", "draw_ps", "abs_ok", "relu_ok", "sp_exp_ok", "sp_ln_ok",
                  "one_plus", "rest_ok", "base_ok"))
        bc_ok = [sem("bc_ok0"), sem("bc_ok1")]
        delta_ok, du_ok, hi_ok, dve_lo = ([sem(f"{n}{c}") for c in range(2 * NQ)] for n in ("delta_ok", "du_ok", "hi_ok", "dve_lo"))
        pool_lo = sem("pool_lo")
        skip_ok, gz_ok, turned_ps = sem("skip_ok"), sem("gz_ok"), sem("turned_ps")
        d_spread, du_spread, exp_done, dbu_done, scan_done, hc_done, y_done = map(
            sem, ("d_spread", "du_spread", "exp_done", "dbu_done", "scan_done", "hc_done", "y_done"))
        row_f_ok = sem("row_f_ok")
        x_stored, row_hot_ok, slot_id_ok, table_ps, y_at_ok, x_at_ok = map(
            sem, ("x_stored", "row_hot_ok", "slot_id_ok", "table_ps", "y_at_ok", "x_at_ok"))
        x2_ok, stats2_ok, std2_ok, rstd2_ok, xn_ok, xnT_ps, xnT_ok, logit_ps = map(
            sem, ("x2_ok", "stats2_ok", "std2_ok", "rstd2_ok", "xn_ok", "xnT_ps", "xnT_ok", "logit_ps"))
        route, mask_ok, rank_ps, rank_out, egap_ok, slots_ok = map(
            sem, ("route", "mask_ok", "rank_ps", "rank_out", "egap_ok", "slots_ok"))
        table_ok, xn1_ok, xnT1_ok = sem("table_ok"), sem("xn1_ok"), sem("xnT1_ok")
        W0_hi_ok, W1_hi_ok, W0_split, W1_split, xT_split = map(sem, ("W0_hi_ok", "W1_hi_ok", "W0_split", "W1_split", "xT_split"))
        gap_ok, cols_ok = sem("gap_ok"), sem("cols_ok")
        x_in = [sem("x_in0"), sem("x_in1")]
        xT_ps, xT_ok, g_ps, u_ps, silu_ok, hid_ok, hidT_ps, hidT_ok, hidT_split, WO_ok, WO_split, y_ps, y_sb = map(
            sem, ("xT_ps", "xT_ok", "g_ps", "u_ps", "silu_ok", "hid_ok", "hidT_ps", "hidT_ok", "hidT_split", "WO_ok", "WO_split",
                  "y_ps", "y_sb"))
        y_out = [sem("y_out0"), sem("y_out1")]
        fetched = [sem(f"fetched{j}") for j in range(NBLK // 2)]
        comb = [sem("comb0"), sem("comb1")]
        wts_ok, scaled = sem("wts_ok"), sem("scaled")
        pool_comb = [sem("pool_comb0"), sem("pool_comb1")]
        stored = sem("stored")

        block = stack.enter_context(nc.Block())

        def part_of(c, m):
            k = m % 2
            return (d_parts, du_parts)[m // 2][:, 2 * c + k, :], (delta, du)[m // 2][c], k

        def upper(eng, copy, c, m):
            parts, src, k = part_of(c, m)
            rows = slice(GRP * k, GRP * (k + 1))
            eng.wait_ge((delta_ok, du_ok)[m // 2][c], 1)
            copy(parts[rows, :], src[rows, :]).then_inc(hi_ok[c], 1)

        def lower(eng, c, m, done):
            parts, src, k = part_of(c, m)
            rows, other = slice(GRP * k, GRP * (k + 1)), slice(GRP * (1 - k), GRP * (2 - k))
            eng.wait_ge(hi_ok[c], m + 1)
            eng.tensor_tensor(parts[other, :], src[rows, :], parts[rows, :], ALU.subtract).then_inc(done, 1)

        def split(eng, W, lo, hi, hi_ok, done, experts):
            for e in experts:
                eng.wait_ge(hi_ok, e + 1)
                eng.tensor_tensor(lo[:, e, :, :].rearrange("p k m -> p (k m)"), W[:, e, :, :].rearrange("p k m -> p (k m)"),
                                  hi[:, e, :, :].rearrange("p k m -> p (k m)"), ALU.subtract).then_inc(done, 1)

        def split_W0(eng, experts):
            split(eng, W0, W0_lo, W0_hi, W0_hi_ok, W0_split, experts)

        def split_W1(eng, experts):
            split(eng, W1, W1_lo, W1_hi, W1_hi_ok, W1_split, experts)

        def rows_hot(eng, q):
            n = TOPK * QBLK
            rf = row_f[:, q, :, :].rearrange("p k t -> p (k t)").rearrange("p (n o) -> p n o", o=1).to_broadcast((P, n, P))
            ri = iota_row[:, :].rearrange("p (o r) -> p o r", o=1).to_broadcast((P, n, P))
            eng.wait_ge(row_f_ok, q + 1)
            eng.tensor_tensor(row_hot[:, q * n:(q + 1) * n, :], ri, rf, ALU.is_equal).then_inc(row_hot_ok, 1)

        def delta_and_du(eng, c):
            eng.wait_ge(sp_ln_ok, c + 1)
            eng.wait_ge(base_ok, c + 1)
            eng.tensor_tensor(delta[c], sp_ln[c], sp_rest[c], ALU.add).then_inc(delta_ok[c], 1)
            eng.wait_ge(delta_ok[c], 1)
            eng.tensor_tensor(du[c], delta[c], u[:, c // 2, c % 2, :], ALU.mult).then_inc(du_ok[c], 1)

        @block.sync
        def _(sp):
            sp.dma_start(ctx_sb, ctx_1024.rearrange("b (r p) d -> p (b r) d", p=P)).then_inc(ld["ctx"], 16)
            sp.dma_start(inw, in_proj_w.rearrange("(h p) d -> p h d", p=P)).then_inc(ld["inw"], 16)
            sp.dma_start(convw[:, :, :], conv_w.rearrange("(h p) k -> p h k", p=P)).then_inc(ld["convw"], 16)
            sp.dma_start(xs[:, :, :], x.rearrange("b (r p) d -> p (b r) d", p=P)).then_inc(ld["x"], 16)
            sp.wait_ge(ld["small"], 16 * 7)
            sp.wait_ge(ld["x"], 16)
            for e in range(E):
                sp.dma_start(W0[:, e, :, :], w0[e].rearrange("(k p) m -> p k m", p=P)).then_inc(ld["w"], 16)
                sp.dma_start(W1[:, e, :, :], w1[e].rearrange("(k p) m -> p k m", p=P)).then_inc(ld["w"], 16)
            sp.wait_ge(pool_lo, 2 + len(POOL_LOWER))
            for c in range(2 * NQ):
                sp.wait_ge(dve_lo[c], 2 if c == 0 else sum(part == c and m is not None for _, part, m in DVE_SPLIT))
            for e in range(E):
                sp.dma_start(WO[:, e, :, :], wo[e].rearrange("(k p) n -> p k n", p=P)).then_inc(ld["w"], 16)
            for q in range(NQ):
                sp.wait_ge(xn1_ok if q else xn_ok, QBLK)
                sp.dma_start(x_rows[q * QT:(q + 1) * QT, :].rearrange("(t p) d -> p t d", p=P),
                             xn[:, q * QBLK:(q + 1) * QBLK, :]).then_inc(x_stored, 16)
            for i in range(2):
                sp.wait_ge(y_out[i], 16 * ((SLOTS + 1 - i) // 2))
            for j in range(NBLK // 2):
                for k in range(TOPK):
                    at = k * TOK + 2 * j * P
                    sp.dma_start(got[k][:, 2 * j:2 * j + 2, :], y_rows[at:at + 2 * P, :].rearrange("(t p) d -> p t d", p=P)).then_inc(fetched[j], 16)
            for i in range(NBLK):
                if i in POOL_BLOCKS:
                    sp.wait_ge(pool_comb[1], POOL_BLOCKS.index(i) + 1)
                else:
                    sp.wait_ge(comb[1], DVE_BLOCKS.index(i) + 1)
                sp.dma_start(out[i // 2, (i % 2) * P:(i % 2 + 1) * P, :], xs[:, i, :]).then_inc(stored, 16)
            sp.wait_ge(stored, 16 * NBLK)

        @block.gpsimd
        def _(pool):
            pool.memset(ident[:, :], 0.0).then_inc(consts, 1)
            pool.memset(spread_f, 0.0).then_inc(consts, 1)
            pool.wait_ge(consts, 2)
            pool.affine_select(out=ident[:, :], in_=ident[:, :], compare_op=ALU.not_equal, fill=1.0, base=0,
                               pattern=[[-1, P]], channel_multiplier=1).then_inc(consts, 1)
            sv = spread_f.rearrange("p (j c n) -> p j c n", j=TPG, c=CH)
            for part in range(2):
                pool.affine_select(out=sv, in_=sv, compare_op=ALU.not_equal, fill=1.0, base=-GRP * part,
                                   pattern=[[-CH, TPG], [-1, CH], [0, DS]], channel_multiplier=1).then_inc(consts, 1)
                pool.wait_ge(consts, 4 + part)
            pool.memset(sum16[:, :, :], 1.0).then_inc(consts, 1)
            pool.memset(ones[:, :], 1.0).then_inc(consts, 1)
            pool.memset(before[:, :], 1.0).then_inc(consts, 1)
            pool.memset(carry[:, :, :], 1.0).then_inc(consts, 1)
            pool.wait_ge(consts, 9)
            pool.affine_select(out=sum16[:, :, :], in_=sum16[:, :, :], compare_op=ALU.is_ge, fill=0.0, base=0,
                               pattern=[[DS * CH, TPH], [-DS, P]], channel_multiplier=1).then_inc(consts, 1)
            pool.affine_select(out=before[:, :], in_=before[:, :], compare_op=ALU.is_gt, fill=0.0, base=0,
                               pattern=[[1, P]], channel_multiplier=-1).then_inc(consts, 1)
            pool.memset(carry[:, :, 0:1], 0.0).then_inc(consts, 1)
            for tab, pattern in ((iota_e, [[0, QBLK], [1, E]]), (iota_c, [[0, 1], [1, COLS]]), (iota_k, [[0, E], [P, NBLK]]),
                                 (iota_s, [[1, SLOTS], [0, E]])):
                pool.iota(tab[:, :, :], pattern=pattern, base=0, channel_multiplier=0,
                          allow_small_or_imprecise_dtypes=True).then_inc(consts, 1)
            pool.iota(iota_row[:, :], pattern=[[1, P]], base=0, channel_multiplier=0,
                      allow_small_or_imprecise_dtypes=True).then_inc(consts, 1)
            pool.wait_ge(consts, 17)
            pool.affine_select(out=sum16[:, :, :], in_=sum16[:, :, :], compare_op=ALU.is_ge, fill=0.0, base=DS - 1,
                               pattern=[[-DS * CH, TPH], [DS, P]], channel_multiplier=-1).then_inc(consts, 1)

            pool.iota(result_id[:, :, :, :], pattern=[[QT, NQ], [TOK, TOPK], [P, QBLK]], base=1, channel_multiplier=1,
                      allow_small_or_imprecise_dtypes=True).then_inc(consts, 1)
            pool.iota(spare_id[:, :], pattern=[[0, 1]], base=TOPK * TOK + 1, channel_multiplier=1,
                      allow_small_or_imprecise_dtypes=True).then_inc(consts, 1)

            pool.sem_inc(hc_done, RING)
            for c in range(2 * NQ):
                pool.wait_ge(relu_ok, c + 1)
                pool.wait_ge(rest_ok, c + 1)
                pool.tensor_tensor(sp_rest[c], sp_relu[c], sp_rest[c], ALU.subtract).then_inc(base_ok, 1)
            pool.wait_ge(base_ok, 2 * NQ)
            for m in range(2):
                lower(pool, 0, m, pool_lo)
                pool.wait_ge(pool_lo, m + 1)


            def times_C(q, at, end):
                pool.wait_ge(bc_ok[q], 2)
                with pool.Fori(0, (end - at) // RING) as t:
                    for i in range(RING):
                        n = RING * t + (at + i)
                        pool.wait_ge(scan_done, n + 1 + AHEAD)
                        pool.wait_ge(y_done, n + 1)
                        pool.tensor_tensor(hC[:, i % 2, :], states[:, i, :], C_rep[:, q, :],
                                           ALU.mult).then_inc(hc_done, 1)

            at = 0
            for k, (after, (c, m)) in enumerate(POOL_LOWER):
                times_C(0, at, after)
                pool.wait_ge(hc_done, RING + after)
                lower(pool, c, m, pool_lo)
                pool.wait_ge(pool_lo, 2 + k + 1)
                at = after
            times_C(0, at, 2 * TPH)
            times_C(1, 2 * TPH, 4 * TPH)

            split_W1(pool, range(E))
            split_W0(pool, range(DVE_W0, E))
            pool.wait_ge(x_stored, 16 * NQ)
            pool.wait_ge(x_at_ok, 1)

            def x_gather(s):
                if s >= 2:
                    pool.wait_ge(xT_ps, s - 1)
                pool.indirect_dma_start(out=x_tile[s % 2], out_offset=None, in_=x_rows,
                                        in_offset=bass.IndirectOffsetOnAxis(ap=x_at[:, s:s + 1], axis=0)).then_inc(x_in[s % 2], 16)

            for s in range(4):
                x_gather(s)
            for s in range(SLOTS):
                if s + 4 < SLOTS:
                    x_gather(s + 4)
                if s:
                    pool.wait_ge(y_out[1 - s % 2], 16 * ((s + 1) // 2))
                pool.wait_ge(y_sb, s + 1)
                pool.indirect_dma_start(out=y_rows, out_offset=bass.IndirectOffsetOnAxis(ap=y_at[:, s:s + 1], axis=0),
                                        in_=y_tile[s % 2], in_offset=None).then_inc(y_out[s % 2], 16)

            for n, i in enumerate(POOL_BLOCKS):
                for k in range(TOPK):
                    pool.wait_ge(scaled, TOPK * n + k + 1)
                    if k:
                        pool.wait_ge(pool_comb[0], n + 1)
                    pool.tensor_tensor(xs[:, i, :], xs[:, i, :], got[k][:, i, :], ALU.add).then_inc(pool_comb[k], 1)

        @block.scalar
        def _(act):
            for v, vec in enumerate((conv_b, dt_proj_b, D)):
                act.dma_start(vec_rows[2 * v:2 * v + 2, :], vec.rearrange("(h p) -> h p", p=P)).then_inc(ld["small"], 16)
            act.dma_start(xproj_sb[:, :], x_proj_w).then_inc(ld["small"], 16)
            act.dma_start(dtw_sb[:, :, :], dt_proj_w.rearrange("(h p) r -> p h r", p=P)).then_inc(ld["small"], 16)
            act.dma_start(Alog_sb[:, :], A_log.rearrange("(j c) n -> j (c n)", c=CH)).then_inc(ld["small"], 16)
            act.dma_start(gate_sb[:, :, :], gate_w.rearrange("(k p) e -> p k e", p=P)).then_inc(ld["small"], 16)
            for i, gv in enumerate((g_xattn, g_ffn)):
                act.dma_start(gates[:, i:i + 1], gv.rearrange("(a n) -> a n", a=1).to_broadcast((P, 1))).then_inc(ld["gates"], 16)
            act.wait_ge(inwT_ps_ok, 1)
            act.activation(inwT, inwT_ps, ACT.Copy).then_inc(inwT_ok, 1)
            for h in range(2):
                act.wait_ge(tapT_ps, h + 1)
                act.activation(tapwT[:, h, :, :].rearrange("p k e -> p (k e)"), bank[6 + h], ACT.Copy).then_inc(tapT_ok, 1)
            act.wait_ge(ld["gates"], 32)
            act.activation(tg[:, :], gates[:, :], ACT.Tanh).then_inc(tanh_ok, 1)
            act.wait_ge(stats_ok, NBLK * 2 + 1)
            act.activation(std[:, 0, :], vare[:, 0, :], ACT.Sqrt).then_inc(std_ok, 1)
            act.wait_ge(cols_ok, 1)

            def exp_table():
                act.activation(scratch[:, :], tg[0:1, 0:1], ACT.Exp).then_inc(table_ok, 1)

            def normed(b):
                act.wait_ge(rstd2_ok, 2)
                for i in range(2 * b, 2 * b + 2):
                    act.activation(xn[:, i, :], xs[:, i, :], ACT.Identity, bias=nmr[:, i:i + 1],
                                   scale=rstd[:, 1, i:i + 1]).then_inc(xn_ok, 1)

            def xnT_out(k):
                act.wait_ge(xnT_ps, k + 1)
                act.activation(xnT[:, k, :], PZ[k][:, :], ACT.Copy).then_inc(xnT_ok, 1)

            def upper_W(W, hi, e, done):
                act.activation(hi[:, e, :, :].rearrange("p k m -> p (k m)"), W[:, e, :, :].rearrange("p k m -> p (k m)"),
                               ACT.Copy).then_inc(done, 1)

            def silu_u(c):
                q, h = divmod(c, 2)
                if q:
                    act.wait_ge(taps_ok[h], DC)
                else:
                    act.wait_ge(conv_ps, c + 1)
                act.activation(u[:, q, h, :], u[:, q, h, :] if q else CONV[c], ACT.Silu, bias=cols[:, 0, h:h + 1]).then_inc(u_ok, 1)

            def silu_z(i):
                act.activation(zs[:, i, :], xs[:, i, :], ACT.Silu, bias=nmr[:, i:i + 1],
                               scale=rstd[:, 0, i:i + 1]).then_inc(zs_ok, 1)

            act.wait_ge(rstd_ok, 2)
            for i in range(2):
                silu_z(i)
            silu_u(0)
            for i in range(2, 7):
                silu_z(i)
            for c in range(1, 2 * NQ):
                silu_u(c)
            silu_z(7)
            act.wait_ge(Alog_ok, 1)
            act.activation(Aexp[:, :], Aexp[:, :], ACT.Exp).then_inc(Aexp_ok, 1)
            for q in range(NQ):
                for c in (2 * q, 2 * q + 1):
                    act.wait_ge(relu_ok, c + 1)
                    act.activation(sp_exp[c], DRAW[c], ACT.Abs, bias=cols[:, 1, c % 2:c % 2 + 1]).then_inc(abs_ok, 1)
                for c in (2 * q, 2 * q + 1):
                    act.wait_ge(abs_ok, c + 1)
                    act.activation(sp_exp[c], sp_exp[c], ACT.Exp, scale=-1.0).then_inc(sp_exp_ok, 1)
            for c in range(2 * NQ):
                act.wait_ge(sp_exp_ok, c + 1)
                act.activation(sp_ln[c], sp_exp[c], ACT.Ln, bias=1.0).then_inc(sp_ln_ok, 1)
            exp_table()
            act_copy = lambda out, in_: act.activation(out, in_, ACT.Copy)
            for n, rep in enumerate((B_rep, C_rep)):
                act.wait_ge(bc_ps, 3 + n)
                act_copy(rep[:, 1, :], BC[1][n]).then_inc(bc_ok[1], 1)
            act.wait_ge(Aneg_ok, 2)
            act.sem_inc(exp_done, AHEAD)

            def decay(at, end):
                with act.Fori(at // 2, end // 2) as t:
                    for i in range(2):
                        n = 2 * t + i
                        act.wait_ge(d_spread, n + 1)
                        act.wait_ge(scan_done, n + 1)
                        act.activation(dA[:, i, :].rearrange("p (b l) -> p b l", b=QB)[:, :, 1:L],
                                       PD[i][:, :].rearrange("p (b l) -> p b l", b=QB)[:, :, 1:L],
                                       ACT.Exp, scale=Aneg[:, bass.ds(n, 1)]).then_inc(exp_done, 1)

            def root(q):
                act.wait_ge(stats2_ok, (q + 1) * (2 * QBLK + 1))
                act.activation(std[:, 1, q * QBLK:(q + 1) * QBLK], vare[:, 1, q * QBLK:(q + 1) * QBLK], ACT.Sqrt).then_inc(std2_ok, 1)

            at = 0
            for after, c, m in ACT_UPPER:
                if after > at:
                    decay(at, after)
                    at = after
                upper(act, act_copy, c, m)
            decay(at, ROOT_AT)
            root(0)
            act.wait_ge(table_ok, 1)
            exp_table()
            decay(ROOT_AT, NORM_AT[0])
            normed(0)
            decay(NORM_AT[0], NORM_AT[1])
            normed(1)
            decay(NORM_AT[1], XNT_AT[0])
            xnT_out(0)
            decay(XNT_AT[0], XNT_AT[1])
            xnT_out(1)
            decay(XNT_AT[1], NQ * 2 * TPH)
            act.wait_ge(ld["w"], 16 * 3 * E)
            act.wait_ge(du_spread, NQ * 2 * TPH)
            act.wait_ge(table_ok, 2)
            act.activation(scratch[:, :], std[0:1, 0, 0:1], ACT.Sqrt).then_inc(table_ok, 1)
            for e in range(6):
                upper_W(W0, W0_hi, e, W0_hi_ok)
            act.wait_ge(turned_ps, NQ * QB)
            for e in range(3):
                upper_W(W1, W1_hi, e, W1_hi_ok)
            root(1)
            act.wait_ge(xnT_ps, 2 * NQ)
            act.activation(xnT[:, 1, :], PZ[1][:, :], ACT.Copy).then_inc(xnT1_ok, 1)
            for e in range(6, E):
                upper_W(W0, W0_hi, e, W0_hi_ok)
            for e in range(3, E):
                if e == E - 1:
                    act.wait_ge(logit_ps, NQ)
                upper_W(W1, W1_hi, e, W1_hi_ok)
            act.wait_ge(gap_ok, 1)
            act.activation(egap[:, :], gap[:, :], ACT.Exp).then_inc(egap_ok, 1)

            act.wait_ge(x_stored, 16 * NQ)

            def xT_out(s, i):
                act.wait_ge(xT_ps, s + 1)
                if not (isinstance(s, int) and s < 2):
                    act.wait_ge(u_ps, s - 1)
                act.activation(xT_hi[i].rearrange("p k t -> p (k t)"), bank[6][:, i * DX:(i + 1) * DX], ACT.Copy).then_inc(xT_ok, 1)

            def silu(s, i):
                act.wait_ge(g_ps, s + 1)
                if not (isinstance(s, int) and s < 2):
                    act.wait_ge(hidT_ps, s - 1)
                act.activation(hid[:, i, :], bank[i][:, :], ACT.Silu).then_inc(silu_ok, 1)

            def hidT_out(s, i):
                act.wait_ge(hidT_ps, s + 1)
                if not (isinstance(s, int) and s < 1):
                    act.wait_ge(y_ps, s)
                act.activation(hidT_hi[:, :, :].rearrange("p k t -> p (k t)"), bank[4 + i], ACT.Copy).then_inc(hidT_ok, 1)

            def WO_out(s):
                expert = act.value_load(slot_tab[0:1, bass.ds(s, 1)], min_val=0, max_val=E - 1)
                if not (isinstance(s, int) and s < 1):
                    act.wait_ge(y_ps, s)
                for h in range(2):
                    cut = slice(2 * h, 2 * h + 2)
                    act.activation(WO_hi[:, cut, :].rearrange("p k n -> p (k n)"),
                                   WO[:, bass.ds(expert, 1), cut, :].rearrange("p o k n -> p (o k n)"), ACT.Copy).then_inc(WO_ok, 1)

            def y_out_of_bank(s, i, reused):
                act.wait_ge(y_ps, s + 1)
                if reused is not None:
                    act.wait_ge(y_out[i], reused)
                act.activation(y_tile[i], bank[7][:, i * DX:(i + 1) * DX], ACT.Copy).then_inc(y_sb, 1)

            def expert_tile(s, i, reused):
                hidT_out(s, i)
                if not (isinstance(s, int) and s + 2 >= SLOTS):
                    xT_out(s + 2, i)
                if not (isinstance(s, int) and s < 1):
                    y_out_of_bank(s - 1, 1 - i, reused)
                if not (isinstance(s, int) and s + 1 >= SLOTS):
                    silu(s + 1, 1 - i)
                    WO_out(s + 1)

            act.wait_ge(slots_ok, 1)
            WO_out(0)
            xT_out(0, 0)
            xT_out(1, 1)
            silu(0, 0)
            for s in range(4):
                expert_tile(s, s % 2, 16 * ((s - 1) // 2) if s > 2 else None)
            with act.Fori(2, (SLOTS - 3) // 2) as t:
                for i in range(2):
                    expert_tile(2 * t + i, i, 16 * t + 16 * (i - 1))
            for s in range(SLOTS - 3, SLOTS):
                expert_tile(s, s % 2, 16 * ((s - 1) // 2))
            y_out_of_bank(SLOTS - 1, (SLOTS - 1) % 2, 16 * ((SLOTS - 1) // 2))
            act.wait_ge(wts_ok, 1)
            for i in POOL_BLOCKS:
                act.wait_ge(fetched[i // 2], 16 * TOPK)
                for k in range(TOPK):
                    act.activation(got[k][:, i, :], got[k][:, i, :], ACT.Copy, scale=wts[:, k, i:i + 1]).then_inc(scaled, 1)

        @block.tensor
        def _(pe):
            pe.wait_ge(consts, 3)
            pe.wait_ge(ld["ctx"], 16)
            for t in range(NBLK):
                pe.transpose(bank[4 + t // 4][:, (t % 4) * P:(t % 4 + 1) * P], ctx_sb[:, t, :], ident[:, :]).then_inc(ctxT_ps, 1)
            pe.wait_ge(ld["inw"], 16)
            for h in range(2):
                mm = pe.transpose(inwT_ps[:, h * P:(h + 1) * P], inw[:, h, :], ident[:, :])
            mm.then_inc(inwT_ps_ok, 1)
            for h in range(2):
                pe.wait_ge(tapw_ok, DC * (h + 1))
                for k in range(DC):
                    mm = pe.transpose(bank[6 + h][:, k * P:(k + 1) * P], tapw[:, h, k, :], ident[:, :])
                mm.then_inc(tapT_ps, 1)
            pe.wait_ge(ctxT_ok, 3)
            pe.wait_ge(inwT_ok, 1)
            for h in range(2):
                pe.matmul(XI[h].rearrange("p (b l) -> p b l", b=QB), inwT[:, h * P:(h + 1) * P], ctxT[:, QB:, DC - 1:],
                          start=True, stop=True).then_inc(xi_ps, 1)
            pe.wait_ge(ld["small"], 16 * 7)
            for h in range(2):
                pe.transpose(xprojT_ps[h], xproj_sb[:, h * P:(h + 1) * P], ident[0:DR + 2 * DS, 0:DR + 2 * DS])
                pe.transpose(dtwT_ps[h], dtw_sb[:, h, :], ident[:, :])
            pe.transpose(cols_ps, vec_rows[:, :], ident[0:6, 0:6])
            pe.transpose(A_ps, Alog_sb[:, :], ident[0:NG * TPG, 0:NG * TPG]).then_inc(smallT_ps, 1)
            for h in range(2):
                pe.wait_ge(tapT_ok, h + 1)
                for k in range(DC):
                    mm = pe.matmul(CONV[h].rearrange("p (b l) -> p b l", b=QB), tapwT[:, h, k, :],
                                   ctxT[:, 0:QB, k:k + L], start=(k == 0), stop=(k == DC - 1))
                mm.then_inc(conv_ps, 1)

            def of_u(w, dest, q, done):
                for h in range(2):
                    mm = pe.matmul(dest, w[h], u[:, q, h, :], start=(h == 0), stop=(h == 1))
                mm.then_inc(done, 1)

            w_dt = [xprojT_dt[:, h, :] for h in range(2)]
            w_B, w_C = ([w[:, h, :, :].rearrange("p c n -> p (c n)") for h in range(2)] for w in (xprojT_B, xprojT_C))

            def delta_raw(q):
                pe.wait_ge(dt_ok, q + 1)
                for h in range(2):
                    pe.matmul(DRAW[2 * q + h], dtwT[:, h, :], dt_lo[:, q, :], start=True, stop=True).then_inc(draw_ps, 1)

            pe.wait_ge(small_ok, 5)
            pe.wait_ge(u_ok, 2)
            of_u(w_dt, DT[0], 0, dt_ps)
            pe.wait_ge(u_ok, 4)
            of_u(w_dt, DT[1], 1, dt_ps)
            pe.wait_ge(Alog_ok, 1)
            delta_raw(0)
            delta_raw(1)
            of_u(w_B, BC[0][0], 0, bc_ps)
            of_u(w_C, BC[0][1], 0, bc_ps)
            of_u(w_B, BC[1][0], 1, bc_ps)
            pe.wait_ge(bc_ok[0], 1)
            of_u(w_C, BC[1][1], 1, bc_ps)

            def spread_tile(g, j, n):
                pe.wait_ge(exp_done, n + 1)
                pe.matmul(PD[j % 2][:, :], spread[:, j, :], d_parts[:, bass.ds(g, 1), :].rearrange("p o t -> p (o t)"),
                          start=True, stop=True).then_inc(d_spread, 1)
                pe.wait_ge(dbu_done, n + 1)
                pe.matmul(PU[j % 2][:, :], spread[:, j, :], du_parts[:, bass.ds(g, 1), :].rearrange("p o t -> p (o t)"),
                          start=True, stop=True).then_inc(du_spread, 1)

            def sum_states(h, j, n):
                pe.wait_ge(hc_done, n + 1 + RING)
                pe.matmul(PY[:, bass.ds(h, 1), :].rearrange("p o t -> p (o t)"), sum16[:, j, :], hC[:, j % 2, :],
                          start=(j == 0), stop=(j == TPH - 1)).then_inc(y_done, 1)

            def half(q, it, last=False, hooks={}):
                if q:
                    pe.wait_ge(gz_ok, it - 1)
                for j in range(TPH):
                    n = it * TPH + j
                    if j + LEAD < TPH or not last:
                        spread_tile(it * 2 + (j + LEAD) // TPG, (j + LEAD) % TPG, n + LEAD)
                    sum_states(it - 2 * q, j, n)
                    if j in hooks:
                        hooks[j]()

            def turn_gz(q):
                pe.wait_ge(gz_ok, 2 * q + 2)
                if q:
                    pe.wait_ge(rank_out, 2)
                for r in range(QB):
                    for l in range(2):
                        for h in range(2):
                            mm = pe.transpose(PZ[r][:, l * DX + h * P:l * DX + (h + 1) * P],
                                              zs[:, q * QBLK + 2 * r + h, l * P:(l + 1) * P], ident[:, :])
                    mm.then_inc(turned_ps, 1)

            def turn_xn(q):
                pe.wait_ge(xn1_ok if q else xn_ok, QBLK)
                for k in range(2):
                    for r in range(QBLK):
                        mm = pe.transpose(PZ[k][:, r * P:(r + 1) * P], xn[:, q * QBLK + r, k * P:(k + 1) * P], ident[:, :])
                    mm.then_inc(xnT_ps, 1)

            def router(q):
                pe.wait_ge(xnT1_ok if q else xnT_ok, 2)
                for r in range(QBLK):
                    for k in range(2):
                        mm = pe.matmul(PZ[1][:, r * E:(r + 1) * E], xnT[:, k, r * P:(r + 1) * P], gate_sb[:, k, :],
                                       start=(k == 0), stop=(k == 1))
                mm.then_inc(logit_ps, 1)

            def ranks(q):
                pe.wait_ge(mask_ok, q + 1)
                m = mask[:, q, :, :].rearrange("p t e -> p (t e)")
                pe.matmul(PZ[0][:, 0:QBLK * E], before[:, :], m, start=True, stop=True)
                pe.matmul(PZ[0][:, 64:64 + QBLK * E], ones[:, :], m, start=True, stop=True).then_inc(rank_ps, 1)

            pe.wait_ge(spread_ok, 1)
            pe.wait_ge(abs_ok, 4)
            pe.wait_ge(bc_ok[0], 2)
            pe.wait_ge(bc_ok[1], 2)
            pe.wait_ge(consts, 18)
            pe.sem_inc(y_done, AHEAD)

            def parts_of(c):
                pe.wait_ge(hi_ok[c], 4)
                pe.wait_ge(pool_lo, 2 + sum(part[0] <= c for _, part in POOL_LOWER))
                pe.wait_ge(dve_lo[c], 2 if c == 0 else sum(part == c and m is not None for _, part, m in DVE_SPLIT))

            parts_of(0)
            for j in range(LEAD):
                spread_tile(0, j, j)
            due = TPH - LEAD - 1
            half(0, 0, hooks={due: lambda: parts_of(1)})
            half(0, 1, hooks={due: lambda: (parts_of(2), parts_of(3))})
            post = {n: (lambda work=work: work(0)) for n, work in zip(PE_POST, (turn_gz, turn_xn, router, ranks))}
            half(1, 2, hooks={n - 2 * TPH: work for n, work in post.items()})
            half(1, 3, last=True, hooks={n - 3 * TPH: work for n, work in post.items()})

            def keep_warm(n):
                for _ in range(n):
                    pe.matmul(PD[0][:, :], ident[:, :], WO[:, 0, 0:2, :].rearrange("p k n -> p (k n)"), start=True, stop=True)

            pe.wait_ge(ld["w"], 16 * 3 * E)
            pe.wait_ge(exp_done, NQ * 2 * TPH + AHEAD)
            turn_gz(1)
            keep_warm(WARM[0])
            turn_xn(1)
            router(1)
            keep_warm(WARM[1])
            ranks(1)
            keep_warm(WARM[2])
            pe.wait_ge(slot_id_ok, 1)
            n = NQ * TOPK * QBLK
            for j in range(n):
                if j % (n // NQ) == 0:
                    pe.wait_ge(row_hot_ok, j // (n // NQ) + 1)
                mm = pe.matmul(PZ[1][:, 0:COLS], row_hot[:, j, :], slot_id[:, j, :], start=(j == 0), stop=(j == n - 1))
            mm.then_inc(table_ps, 1)
            keep_warm(WARM[3])

            pe.wait_ge(slots_ok, 1)
            pe.wait_ge(ld["w"], 16 * 3 * E)

            def x_turn(s, i, loaded):
                pe.wait_ge(x_in[i], loaded)
                if not (isinstance(s, int) and s < 1):
                    pe.wait_ge(xT_split, s)
                for k in range(2):
                    mm = pe.transpose(bank[6][:, i * DX + k * P:i * DX + (k + 1) * P], x_tile[i][:, k * P:(k + 1) * P], ident[:, :])
                mm.then_inc(xT_ps, 1)

            def product(hi, lo, dest, i, expert, done):
                terms = [(x, w, k) for x, w in ((xT_hi, hi), (xT_hi, lo), (xT_lo, hi)) for k in range(2)]
                for n, (x, w, k) in enumerate(terms):
                    mm = pe.matmul(dest[i][:, :], x[i][:, k, :], w[:, bass.ds(expert, 1), k, :].rearrange("p o m -> p (o m)"),
                                   start=(n == 0), stop=(n == len(terms) - 1))
                mm.then_inc(done, 1)

            def gate(s, i, expert):
                pe.wait_ge(xT_split, s + 1)
                if not (isinstance(s, int) and s < 2):
                    pe.wait_ge(silu_ok, s - 1)
                product(W0_hi, W0_lo, bank[0:2], i, expert, g_ps)

            def up(s, i, expert):
                if not (isinstance(s, int) and s < 2):
                    pe.wait_ge(hid_ok, s - 1)
                product(W1_hi, W1_lo, bank[2:4], i, expert, u_ps)

            def hid_turn(s, i):
                pe.wait_ge(hid_ok, s + 1)
                if not (isinstance(s, int) and s < 2):
                    pe.wait_ge(hidT_split, s - 1)
                for k in range(4):
                    mm = pe.transpose(bank[4 + i][:, k * P:(k + 1) * P], hid[:, i, k * P:(k + 1) * P], ident[:, :])
                mm.then_inc(hidT_ps, 1)

            def down(s, i):
                pe.wait_ge(hidT_ok, s + 1)
                pe.wait_ge(WO_ok, 2 * s + 2)
                if not (isinstance(s, int) and s < 1):
                    pe.wait_ge(y_sb, s)
                for n, (x, w) in enumerate(((hidT_hi, WO_hi), (hidT_hi, WO_lo), (hidT_lo, WO_hi))):
                    if n == 1:
                        pe.wait_ge(WO_split, 2 * s + 2)
                    if n == 2:
                        pe.wait_ge(hidT_split, s + 1)
                    for k in range(4):
                        mm = pe.matmul(bank[7][:, i * DX:(i + 1) * DX], x[:, k, :], w[:, k, :],
                                       start=(n == 0 and k == 0), stop=(n == 2 and k == 3))
                mm.then_inc(y_ps, 1)

            def expert_of(s):
                return pe.value_load(slot_tab[0:1, bass.ds(s, 1)], min_val=0, max_val=E - 1)

            def step(s, i, loaded, turn=True, nxt=True):
                if nxt:
                    follows = expert_of(s + 1)
                if turn:
                    x_turn(s + 2, i, loaded)
                hid_turn(s, i)
                if nxt:
                    gate(s + 1, 1 - i, follows)
                    up(s + 1, 1 - i, follows)
                down(s, i)

            first = expert_of(0)
            x_turn(0, 0, 16)
            pe.wait_ge(W0_split, E)
            gate(0, 0, first)
            x_turn(1, 1, 16)
            pe.wait_ge(W1_split, E)
            up(0, 0, first)
            step(0, 0, 32)
            step(1, 1, 32)
            with pe.Fori(0, (SLOTS - 5) // UNROLL) as t:
                for j in range(UNROLL):
                    step(UNROLL * t + (2 + j), j % 2, 8 * UNROLL * t + (48 + 16 * (j // 2)))
            step(SLOTS - 3, 0, 16 * ((SLOTS + 1) // 2))
            step(SLOTS - 2, 1, 0, turn=False)
            step(SLOTS - 1, 0, 0, turn=False, nxt=False)

        @block.vector
        def _(dve):
            dve.memset(ctxT[:, :, 0:DC - 1], 0.0).then_inc(ctxT_ok, 1)
            dve.wait_ge(ld["inw"], 16)
            dve.wait_ge(ld["convw"], 16)
            for h in range(2):
                for k in range(DC):
                    dve.tensor_scalar(tapw[:, h, k, :], inw[:, h, :], convw[:, h, k:k + 1], None, ALU.mult).then_inc(tapw_ok, 1)
            for q in range(NQ):
                dve.wait_ge(ctxT_ps, 4 * (q + 1))
                dve.tensor_copy(ctxT[:, q * QB:(q + 1) * QB, DC - 1:], bank[4 + q].rearrange("p (b l) -> p b l", b=QB)).then_inc(ctxT_ok, 1)
            dve.wait_ge(ld["x"], 16)
            for i in range(NBLK):
                dve.bn_stats(stats[:, 0, i, :], xs[:, i, :]).then_inc(stats_ok, 1)
            dve.wait_ge(stats_ok, NBLK)
            for i in range(NBLK):
                dve.bn_aggr(mv[:, 0, i, :], stats[:, 0, i, :]).then_inc(stats_ok, 1)
            dve.wait_ge(stats_ok, 2 * NBLK)
            dve.tensor_scalar(vare[:, 0, :], mv[:, 0, :, 1], EPS, None, ALU.add).then_inc(stats_ok, 1)
            def tap(h, back):
                q_u = u[:, 1, h, :].rearrange("p (b l) -> p b l", b=QB)
                xi = XI[h].rearrange("p (b l) -> p b l", b=QB)
                w = convw[:, h, DC - 1 - back:DC - back]
                if back == 0:
                    dve.wait_ge(xi_ps, h + 1)
                    dve.tensor_scalar(q_u, xi, w, None, ALU.mult).then_inc(taps_ok[h], 1)
                else:
                    dve.wait_ge(taps_ok[h], back)
                    dve.scalar_tensor_tensor(out=q_u[:, :, back:], in0=xi[:, :, 0:L - back], scalar=w, in1=q_u[:, :, back:],
                                             op0=ALU.mult, op1=ALU.add).then_inc(taps_ok[h], 1)

            tap(0, 0)
            tap(1, 0)
            dve.wait_ge(std_ok, 1)
            dve.reciprocal(rstd[:, 0, :], std[:, 0, :]).then_inc(rstd_ok, 1)
            dve.wait_ge(rstd_ok, 1)
            dve.scalar_tensor_tensor(out=nmr[:, :], in0=mv[:, 0, :, 0], scalar=-1.0, in1=rstd[:, 0, :],
                                     op0=ALU.mult, op1=ALU.mult).then_inc(rstd_ok, 1)
            dve.wait_ge(smallT_ps, 1)
            dve.tensor_copy(cols[:, :, :].rearrange("p v h -> p (v h)"), cols_ps).then_inc(cols_ok, 1)
            for h in range(2):
                dve.tensor_copy(xprojT_dt[:, h, :], xprojT_ps[h][:, 0:DR])
                for n, w in enumerate((xprojT_B, xprojT_C)):
                    src = xprojT_ps[h][:, DR + n * DS:DR + (n + 1) * DS].rearrange("p (o n) -> p o n", o=1).to_broadcast((P, CH, DS))
                    dve.tensor_copy(w[:, h, :, :], src).then_inc(small_ok, 1)
            dve.tensor_copy(dtwT[:, :, :].rearrange("r h e -> r (h e)"), bank[3][0:DR, P:3 * P]).then_inc(small_ok, 1)
            dve.tensor_copy(Aexp[:, :], A_ps).then_inc(Alog_ok, 1)
            for back in range(1, DC):
                for h in range(2):
                    tap(h, back)
            dve.wait_ge(consts, 5)
            dve.tensor_copy(spread[:, :, :].rearrange("p j m -> p (j m)"), spread_f).then_inc(spread_ok, 1)

            def dt_out(q):
                dve.wait_ge(dt_ps, q + 1)
                dve.tensor_copy(dt_lo[:, q, :], DT[q]).then_inc(dt_ok, 1)

            def bc_out(n):
                dve.wait_ge(bc_ps, n + 1)
                dve.tensor_copy((B_rep, C_rep)[n][:, 0, :], BC[0][n]).then_inc(bc_ok[0], 1)

            def relu(c):
                dve.wait_ge(draw_ps, c + 1)
                dve.tensor_scalar(sp_relu[c], DRAW[c], cols[:, 1, c % 2:c % 2 + 1], 0.0, ALU.add, ALU.max).then_inc(relu_ok, 1)

            def rounding(q):
                for c in (2 * q, 2 * q + 1):
                    dve.wait_ge(sp_exp_ok, c + 1)
                    dve.tensor_scalar(sp_rest[c], sp_exp[c], 1.0, None, ALU.add).then_inc(one_plus, 1)
                for c in (2 * q, 2 * q + 1):
                    dve.wait_ge(one_plus, c + 1)
                    dve.scalar_tensor_tensor(out=sp_rest[c], in0=sp_rest[c], scalar=1.0, in1=sp_exp[c],
                                             op0=ALU.subtract, op1=ALU.subtract).then_inc(rest_ok, 1)

            dt_out(0)
            dt_out(1)
            relu(0)
            relu(1)
            dve.wait_ge(Aexp_ok, 1)
            for k in range(NQ):
                dve.tensor_scalar(Aneg[:, k * NG * TPG:(k + 1) * NG * TPG], Aexp[:, :], -1.0, None, ALU.mult).then_inc(Aneg_ok, 1)
            relu(2)
            relu(3)
            rounding(0)
            bc_out(0)
            rounding(1)
            delta_and_du(dve, 0)
            for m in range(4):
                upper(dve, dve.tensor_copy, 0, m)
            bc_out(1)
            for m in range(2, 4):
                lower(dve, 0, m, dve_lo[0])
            delta_and_du(dve, 1)
            dve.wait_ge(sp_ln_ok, 4)
            dve.wait_ge(rest_ok, 4)
            dve.memset(dA[:, :, :].rearrange("p i (b l) -> p (i b) l", b=QB)[:, :, 0:1], 0.0).then_inc(scan_done, AHEAD)

            def drive(q, j, n):
                dve.wait_ge(du_spread, n + 1)
                dve.wait_ge(hc_done, n + 1)
                dve.tensor_tensor(states[:, j, :], PU[j % 2][:, :], B_rep[:, q, :], ALU.mult).then_inc(dbu_done, 1)

            def scan(j, n):
                dve.wait_ge(exp_done, n + 1 + AHEAD)
                dve.wait_ge(dbu_done, n + 1 + AHEAD)
                dve.tensor_tensor_scan(states[:, j, :], dA[:, j % 2, :], states[:, j, :], 0.0,
                                       ALU.mult, ALU.add).then_inc(scan_done, 1)

            def drive_and_scan(q, j, n):
                if q < NQ:
                    drive(q, (j + 1) % RING, n + 1)
                scan(j, n)

            def tiles_to(q, at, end):
                last = (q + 1) * 2 * TPH - 1
                turns = (min(end, last) - at) // RING
                if turns:
                    with dve.Fori(0, turns) as t:
                        for i in range(RING):
                            drive_and_scan(q, (at + i) % RING, RING * t + (at + i))
                for n in range(at + RING * turns, end):
                    drive_and_scan(q + (n == last), n % RING, n)
                return end

            def run(q, at, *work):
                for after, do in work:
                    at = tiles_to(q, at, after)
                    do()
                tiles_to(q, at, (q + 1) * 2 * TPH)

            def gated(q, h, it):
                dve.wait_ge(y_done, AHEAD + (it + 1) * TPH)
                if it:
                    dve.wait_ge(gz_ok, it)
                yb = PY[:, bass.ds(h, 1), :].rearrange("p o t -> p (o t)")
                uh = u[:, q, bass.ds(h, 1), :].rearrange("p o t -> p (o t)")
                dve.scalar_tensor_tensor(out=skip[:, :], in0=uh, scalar=cols[:, 2, bass.ds(h, 1)], in1=yb,
                                         op0=ALU.mult, op1=ALU.add).then_inc(skip_ok, 1)
                dve.wait_ge(skip_ok, it + 1)
                zh = zs[:, :, :].rearrange("p (r h) l -> p h r l", h=2)[:, bass.ds(h, 1), 2 * q:2 * q + 2, :].rearrange("p o r l -> p (o r) l")
                dve.tensor_tensor(zh, skip[:, :].rearrange("p (r l) -> p r l", r=QB), zh, ALU.mult).then_inc(gz_ok, 1)

            def residual(q, r):
                b = q * QB + r
                dve.wait_ge(turned_ps, b + 1)
                xb = xs[:, 2 * b:2 * b + 2, :].rearrange("p t d -> p (t d)")
                dve.scalar_tensor_tensor(out=xb, in0=PZ[r][:, :], scalar=tg[:, 0:1], in1=xb,
                                         op0=ALU.mult, op1=ALU.add).then_inc(x2_ok, 1)
                dve.wait_ge(x2_ok, b + 1)
                for i in range(2 * b, 2 * b + 2):
                    dve.bn_stats(stats[:, 1, i, :], xs[:, i, :]).then_inc(stats2_ok, 1)

            def variance(q):
                base = q * (2 * QBLK + 1)
                cut = slice(q * QBLK, (q + 1) * QBLK)
                dve.wait_ge(stats2_ok, base + QBLK)
                for i in range(q * QBLK, (q + 1) * QBLK):
                    dve.bn_aggr(mv[:, 1, i, :], stats[:, 1, i, :]).then_inc(stats2_ok, 1)
                dve.wait_ge(stats2_ok, base + 2 * QBLK)
                dve.tensor_scalar(vare[:, 1, cut], mv[:, 1, cut, 1], EPS, None, ALU.add).then_inc(stats2_ok, 1)

            def normed(q):
                cut = slice(q * QBLK, (q + 1) * QBLK)
                dve.wait_ge(std2_ok, q + 1)
                dve.reciprocal(rstd[:, 1, cut], std[:, 1, cut]).then_inc(rstd2_ok, 1)
                dve.wait_ge(rstd2_ok, 2 * q + 1)
                dve.scalar_tensor_tensor(out=nmr[:, cut], in0=mv[:, 1, cut, 0], scalar=-1.0, in1=rstd[:, 1, cut],
                                         op0=ALU.mult, op1=ALU.mult).then_inc(rstd2_ok, 1)

            steps = [0]

            def link(ins):
                ins.then_inc(route, 1)
                steps[0] += 1
                dve.wait_ge(route, steps[0])

            def best_two(q):
                cut = slice(q * QBLK, (q + 1) * QBLK)
                dve.wait_ge(logit_ps, q + 1)
                link(dve.tensor_copy(logits[:, cut, :].rearrange("p t e -> p (t e)"), PZ[1][:, 0:QBLK * E]))
                for r in range(QBLK):
                    ins = dve.max(top[:, q * QBLK + r, :], logits[:, q * QBLK + r, :])
                    if r < QBLK - 1:
                        ins.then_inc(route, 1)
                        steps[0] += 1
                link(ins)
                for r in range(QBLK):
                    ins = dve.max_index(topi[:, q * QBLK + r, :], top[:, q * QBLK + r, :], logits[:, q * QBLK + r, :])
                    if r < QBLK - 1:
                        ins.then_inc(route, 1)
                        steps[0] += 1
                link(ins)
                link(dve.tensor_copy(topf[:, cut, :], topi[:, cut, 0:TOPK]))
                for k in range(TOPK):
                    ins = dve.tensor_tensor(hot[:, q, k, :, :], iota_e[:, :, :], topf[:, cut, k:k + 1].to_broadcast((P, QBLK, E)), ALU.is_equal)
                    if k == 0:
                        ins.then_inc(route, 1)
                        steps[0] += 1
                link(ins)
                dve.tensor_tensor(mask[:, q, :, :], hot[:, q, 0, :, :], hot[:, q, 1, :, :], ALU.add).then_inc(mask_ok, 1)

            def mark(ins):
                ins.then_inc(route, 1)
                steps[0] += 1
                return steps[0]

            def need(step):
                dve.wait_ge(route, step)

            def places(q):
                last = q == NQ - 1
                dve.wait_ge(rank_ps, q + 1)
                dve.wait_ge(consts, 20)
                sums, rk, hot_q = blocksum[:, q, :, :], rank[:, q, :, :], picked[:, q, :, :, :]
                earlier = count[:, 0, :].rearrange("p (o e) -> p o e", o=1).to_broadcast((P, QBLK, E))
                n = NQ * TOPK * QBLK
                of_n = lambda t: t[:, :, :, :].rearrange("p q k t -> p (q k t)")
                dve.tensor_copy(sums, PZ[0][:, 64:64 + QBLK * E].rearrange("p (t e) -> p e t", e=E)).then_inc(rank_out, 1)
                in_bank = PZ[0][:, 0:QBLK * E].rearrange("p (t e) -> p t e", e=E)
                if last:
                    dve.tensor_tensor(rk, in_bank, earlier, ALU.add).then_inc(rank_out, 1)
                else:
                    dve.tensor_copy(rk, in_bank).then_inc(rank_out, 1)
                dve.wait_ge(rank_out, 2 * q + 1)
                up = mark(dve.tensor_tensor_scan(upto[:, q, :, :].rearrange("p e t -> p (e t)"), carry[:, :, :].rearrange("p e t -> p (e t)"),
                                                 sums.rearrange("p e t -> p (e t)"), 0.0, ALU.mult, ALU.add))
                need(up)
                if last:
                    counted = mark(dve.tensor_tensor(count[:, 1, :], upto[:, q, :, QBLK - 1], count[:, 0, :], ALU.add))
                else:
                    counted = mark(dve.tensor_copy(count[:, 0, :], upto[:, q, :, QBLK - 1]))
                before_block = mark(dve.tensor_tensor(sums, upto[:, q, :, :], sums, ALU.subtract))
                if last:
                    need(counted)
                    cnt = count[:, 1, :].rearrange("p (e o) -> p e o", o=1).to_broadcast((P, E, NBLK))
                    exceeded = mark(dve.tensor_tensor(over[:, :, :], cnt, iota_k[:, :, :], ALU.is_gt))
                need(before_block)
                dve.wait_ge(rank_out, 2 * q + 2)
                ranked = mark(dve.tensor_tensor(rk, rk, sums.rearrange("p e t -> p t e"), ALU.add))
                if last:
                    need(exceeded)
                    tiled = mark(dve.tensor_reduce(tiles[:, :], over[:, :, :], AX_X, ALU.add))
                need(ranked)
                for k in range(TOPK):
                    chosen = mark(dve.tensor_tensor(picked[:, q, k, :, :], hot[:, q, k, :, :], rk, ALU.mult))
                if last:
                    need(tiled)
                    ends = mark(dve.tensor_tensor_scan(tile_end[:, :], ones[:, 0:E], tiles[:, :], 0.0, ALU.mult, ALU.add))
                need(chosen)
                flat = lambda t: t[:, q, :, :].rearrange("p k t -> p (k t)")
                summed = mark(dve.tensor_reduce(flat(rank_f), hot_q.rearrange("p k t e -> p (k t) e"), AX_X, ALU.add))
                if last:
                    need(ends)
                    starts = mark(dve.tensor_tensor(first_slot[:, :], tile_end[:, :], tiles[:, :], ALU.subtract))
                need(summed)
                whole = mark(dve.tensor_copy(rank_i[:, q, :, :], rank_f[:, q, :, :]))
                if last:
                    need(starts)
                    hot_n = hot[:, :, :, :, :].rearrange("p q k t e -> p (q k t) e")
                    first = mark(dve.tensor_tensor(first_of[:, :, :], hot_n, first_slot[:, :].rearrange("p (o e) -> p o e", o=1).to_broadcast((P, n, E)), ALU.mult))
                need(whole)
                in_tile = mark(dve.tensor_scalar(row_i[:, q, :, :], rank_i[:, q, :, :], P - 1, None, ALU.bitwise_and))
                before_it = mark(dve.tensor_scalar(tile_i[:, q, :, :], rank_i[:, q, :, :], P.bit_length() - 1, None, ALU.logical_shift_right))
                if last:
                    need(first)
                    slots = mark(dve.tensor_reduce(slot_of[:, :], first_of[:, :, :], AX_X, ALU.add))
                need(before_it)
                before_it = mark(dve.tensor_copy(rank_f[:, q, :, :], tile_i[:, q, :, :]))
                dve.tensor_copy(row_f[:, q, :, :], row_i[:, q, :, :]).then_inc(row_f_ok, 1)
                if last:
                    need(max(slots, before_it))
                    link(dve.tensor_tensor(slot_of[:, :], slot_of[:, :], of_n(rank_f), ALU.add))
                    wide = lambda t: t.rearrange("p (n o) -> p n o", o=1).to_broadcast((P, n, COLS))
                    link(dve.tensor_tensor(slot_id[:, :, :], iota_c[:, :, :].to_broadcast((P, n, COLS)), wide(slot_of[:, :]), ALU.is_equal))
                    dve.tensor_tensor(slot_id[:, :, :], slot_id[:, :, :], wide(of_n(result_id)), ALU.mult).then_inc(slot_id_ok, 1)

            dve.sem_inc(dbu_done, AHEAD)
            drive(0, 0, 0)
            split_c = [(after, lambda c=c, m=m: delta_and_du(dve, c) if m is None else lower(dve, c, m, dve_lo[c]))
                       for after, c, m in DVE_SPLIT]
            run(0, 0, *sorted([*split_c, (GATE_AT[0], lambda: gated(0, 0, 0))], key=lambda w: w[0]))
            run(1, 2 * TPH, (GATE_AT[1], lambda: gated(0, 1, 1)), (RESIDUAL_AT[0], lambda: residual(0, 0)),
                (RESIDUAL_AT[1], lambda: residual(0, 1)), (VARIANCE_AT, lambda: variance(0)), (RSTD_AT, lambda: normed(0)),
                (GATE_AT[2], lambda: gated(1, 0, 2)),
                (BEST_AT, lambda: best_two(0)), (PLACE_AT, lambda: places(0)))
            gated(1, 1, 3)
            residual(1, 0)
            residual(1, 1)
            variance(1)
            normed(1)
            for i in range(QBLK, NBLK):
                dve.tensor_scalar(xn[:, i, :], xs[:, i, :], mv[:, 1, i, 0:1], rstd[:, 1, i:i + 1],
                                  ALU.subtract, ALU.mult).then_inc(xn1_ok, 1)
            dve.wait_ge(xnT_ps, 2 * NQ - 1)
            dve.tensor_copy(xnT[:, 0, :], PZ[0][:, :]).then_inc(xnT1_ok, 1)
            split_W0(dve, range(DVE_EARLY))
            best_two(1)
            rows_hot(dve, 0)
            places(1)
            rows_hot(dve, 1)

            dve.tensor_tensor(gap[:, :], top[:, :, 1], top[:, :, 0], ALU.subtract).then_inc(gap_ok, 1)
            link(dve.tensor_tensor(ended[:, :, :], iota_s[:, :, :],
                                   tile_end[:, :].rearrange("p (o e) -> p o e", o=1).to_broadcast((P, SLOTS, E)), ALU.is_ge))
            link(dve.tensor_reduce(slot_f[:, :], ended[:, :, :], AX_X, ALU.add))
            link(dve.tensor_scalar(slot_f[:, :], slot_f[:, :], float(E - 1), None, ALU.min))
            dve.tensor_copy(slot_tab[:, :], slot_f[:, :]).then_inc(slots_ok, 1)
            split_W0(dve, range(DVE_EARLY, DVE_MIDDLE))
            dve.wait_ge(table_ps, 1)
            link(dve.tensor_scalar(spare[:, :], PZ[1][:, 0:COLS], 0.0, spare_id[:, 0:1], ALU.is_equal, ALU.mult))
            dve.scalar_tensor_tensor(out=y_at[:, :], in0=PZ[1][:, 0:COLS], scalar=-1.0, in1=spare[:, :],
                                     op0=ALU.add, op1=ALU.add).then_inc(y_at_ok, 1)
            dve.wait_ge(y_at_ok, 1)
            dve.tensor_scalar(x_at[:, :], y_at[:, :], TOK - 1, None, ALU.bitwise_and).then_inc(x_at_ok, 1)
            dve.wait_ge(egap_ok, 1)
            link(dve.tensor_scalar(eden[:, :], egap[:, :], 1.0, None, ALU.add))
            link(dve.reciprocal(eden[:, :], eden[:, :]))
            link(dve.tensor_scalar(wts[:, 0, :], eden[:, :], tg[:, 1:2], None, ALU.mult))
            dve.tensor_tensor(wts[:, 1, :], wts[:, 0, :], egap[:, :], ALU.mult).then_inc(wts_ok, 1)

            split_W0(dve, range(DVE_MIDDLE, DVE_W0))

            def split_x(s, i):
                dve.wait_ge(xT_ok, s + 1)
                dve.tensor_tensor(xT_lo[i].rearrange("p k t -> p (k t)"), bank[6][:, i * DX:(i + 1) * DX],
                                  xT_hi[i].rearrange("p k t -> p (k t)"), ALU.subtract).then_inc(xT_split, 1)

            def hidden(s, i):
                dve.wait_ge(silu_ok, s + 1)
                dve.wait_ge(u_ps, s + 1)
                dve.tensor_tensor(hid[:, i, :], bank[2 + i][:, :], hid[:, i, :], ALU.mult).then_inc(hid_ok, 1)

            def split_hidT(s, i):
                dve.wait_ge(hidT_ok, s + 1)
                dve.tensor_tensor(hidT_lo[:, :, :].rearrange("p k t -> p (k t)"), bank[4 + i],
                                  hidT_hi[:, :, :].rearrange("p k t -> p (k t)"), ALU.subtract).then_inc(hidT_split, 1)

            def split_WO(s):
                expert = dve.value_load(slot_tab[0:1, bass.ds(s, 1)], min_val=0, max_val=E - 1)
                for h in range(2):
                    cut = slice(2 * h, 2 * h + 2)
                    dve.wait_ge(WO_ok, 2 * s + h + 1)
                    dve.tensor_tensor(WO_lo[:, cut, :].rearrange("p k n -> p (k n)"),
                                      WO[:, bass.ds(expert, 1), cut, :].rearrange("p o k n -> p (o k n)"),
                                      WO_hi[:, cut, :].rearrange("p k n -> p (k n)"), ALU.subtract).then_inc(WO_split, 1)

            split_x(0, 0)
            split_x(1, 1)
            hidden(0, 0)
            with dve.Fori(0, (SLOTS - 3) // 2) as t:
                for i in range(2):
                    s = 2 * t + i
                    split_WO(s)
                    split_hidT(s, i)
                    split_x(s + 2, i)
                    hidden(s + 1, 1 - i)
            for s in range(SLOTS - 3, SLOTS):
                split_WO(s)
                split_hidT(s, s % 2)
                if s + 2 < SLOTS:
                    split_x(s + 2, s % 2)
                if s + 1 < SLOTS:
                    hidden(s + 1, (s + 1) % 2)

            dve.wait_ge(wts_ok, 1)
            for n, i in enumerate(DVE_BLOCKS):
                dve.wait_ge(fetched[i // 2], 16 * TOPK)
                for k in range(TOPK):
                    if k:
                        dve.wait_ge(comb[0], n + 1)
                    dve.scalar_tensor_tensor(out=xs[:, i, :], in0=got[k][:, i, :], scalar=wts[:, k, i:i + 1],
                                             in1=xs[:, i, :], op0=ALU.mult, op1=ALU.add).then_inc(comb[k], 1)


INPUTS = ("x", "ctx_1024", "g_xattn", "g_ffn", "L0_xattn_in_proj_w", "L0_xattn_conv_w", "L0_xattn_conv_b",
          "L0_xattn_x_proj_w", "L0_xattn_dt_proj_w", "L0_xattn_dt_proj_b", "L0_xattn_A_log", "L0_xattn_D",
          "L0_ffn_gate_w", "L0_ffn_w0", "L0_ffn_w1", "L0_ffn_wo")


def kernel(**inputs):
    import concourse.bacc as bacc
    from concourse.bass_utils import run_bass_kernel_spmd

    nc = bacc.Bacc("TRN2", target_bir_lowering=False, num_devices=1)
    arrays, args = {}, []
    for name in INPUTS:
        a = np.ascontiguousarray(inputs[name])
        arrays["in_" + name] = a
        args.append(nc.dram_tensor("in_" + name, a.shape, mybir.dt.from_np(a.dtype), kind="ExternalInput").ap())
    out = nc.dram_tensor("out", (B, L, DX), F32, kind="ExternalOutput").ap()
    build(nc, *args, out)
    result = run_bass_kernel_spmd(nc, [arrays], core_ids=[0])
    return result.results[0]["out"]
```
